# Optimizing a Trainium2 kernel written in Bass

```python
import numpy as np
import jax
import jax.numpy as jnp

def _softmax(x, axis=-1):
    return jax.nn.softmax(x, axis=axis)

def _gelu(x):
    return jax.nn.gelu(x, approximate=True)

def _silu(x):
    return jax.nn.silu(x)

def _sigmoid(x):
    return jax.nn.sigmoid(x)

def _layernorm(x, axis=-1, eps=1e-05):
    m = jnp.mean(x, axis=axis, keepdims=True)
    v = jnp.var(x, axis=axis, keepdims=True)
    return (x - m) / jnp.sqrt(v + eps)

def _scatter_add(tgt, idx, src, axis=0):
    return tgt.at[idx].add(src)

def _segment_sum(src, seg, n):
    return jax.ops.segment_sum(src, seg, n)
kernel_name = 'mk_xattn_seq_d2_seqx_r4_1b2e32'

def setup_inputs(seed: int=0):
    np.random.seed(seed)
    _w = jnp.asarray

    def _rec_inputs():
        import jax
        import jax.numpy as jnp
        _rk = jax.random.key(seed)
        x = -0.0005146 + 1 * jax.random.normal(jax.random.fold_in(_rk, 1), (16, 128, 512), jnp.float32)
        _lenS = 128 - jax.random.randint(jax.random.fold_in(_rk, 7), (16,), 0, max(1, 128 // 4) + 1, jnp.int32)
        _lenS2 = 128 - jax.random.randint(jax.random.fold_in(_rk, 8), (16,), 0, max(1, 128 // 4) + 1, jnp.int32)
        _ctx_2048P = jax.random.normal(jax.random.fold_in(_rk, 11), (16, 16, 512), jnp.float32)
        _ctx_2048c = jax.random.dirichlet(jax.random.fold_in(_rk, 511), 0.3 * jnp.ones((16,), jnp.float32), (16, 128))
        _ctx_2048t = jnp.einsum('bsk,bkd->bsd', _ctx_2048c, _ctx_2048P)
        _ctx_2048t = _ctx_2048t * jax.lax.rsqrt(jnp.mean(jnp.square(_ctx_2048t)) + 1e-12) * 0.953939
        ctx_2048 = -0.000392918 + 0.999932 * (_ctx_2048t + 0.3 * jax.random.normal(jax.random.fold_in(_rk, 611), (16, 128, 512), jnp.float32))
        _validS = jnp.arange(128)[None, :] < _lenS[:, None]
        _validS2 = jnp.arange(128)[None, :] < _lenS2[:, None]
        _causal = jnp.tril(jnp.ones((128, 128), dtype=bool))
        mask_BxS2_ik0 = jnp.where(jnp.broadcast_to(_validS2[:, :], (16, 128)), 0, 1).astype(jnp.int32)
        mask_Bx1xSxS2_ff0 = jnp.where(jnp.ones((16, 1, 128, 128), dtype=bool), 0.0, -1000000000.0).astype(jnp.float32)
        return (x, ctx_2048, mask_BxS2_ik0, mask_Bx1xSxS2_ff0)
    x, ctx_2048, mask_BxS2_ik0, mask_Bx1xSxS2_ff0 = _rec_inputs()

    def _L0_xattn_setup():
        import jax, jax.numpy as jnp
        import numpy as np
        B, P, K, H, NH = (4, 512, 64, 512, 16)
        DH = H // NH
        EPS = 1e-06

        def rmsnorm(x, w):
            var = jnp.mean(jnp.square(x), axis=-1, keepdims=True)
            return x * jax.lax.rsqrt(var + EPS) * w
        key = jax.random.key(seed)
        ks = jax.random.split(key, 12)
        s = 0.02
        return {'x': jax.random.normal(ks[0], (B, P, H), jnp.float32), 'latents': jax.random.normal(ks[1], (B, K, H), jnp.float32), 'attention_mask': jax.random.randint(ks[2], (B, P), 0, 2, jnp.int32), 'q_w': s * jax.random.normal(ks[3], (H, H), jnp.float32), 'q_b': jnp.zeros((H,), jnp.float32), 'kv_w': s * jax.random.normal(ks[4], (H, 2 * H), jnp.float32), 'kv_b': jnp.zeros((2 * H,), jnp.float32), 'out_w': s * jax.random.normal(ks[5], (H, H), jnp.float32), 'out_b': jnp.zeros((H,), jnp.float32), 'postnorm_w': jnp.ones((H,), jnp.float32), 'mlp_w1': s * jax.random.normal(ks[6], (H, 4 * H), jnp.float32), 'mlp_b1': jnp.zeros((4 * H,), jnp.float32), 'mlp_w2': s * jax.random.normal(ks[7], (4 * H, H), jnp.float32), 'mlp_b2': jnp.zeros((H,), jnp.float32)}
    _L0_xattn_all = _L0_xattn_setup()
    _L0_xattn_in = {k: v for k, v in _L0_xattn_all.items() if k in ('q_w', 'q_b', 'kv_w', 'kv_b', 'out_w', 'out_b', 'postnorm_w', 'mlp_w1', 'mlp_b1', 'mlp_w2', 'mlp_b2')}
    del _L0_xattn_all

    def _L1_xattn_setup():
        import jax, jax.numpy as jnp
        import numpy as np
        H = 512
        NH = 32
        KVH = 8
        HD = H // NH
        GROUPS = NH // KVH
        EPS = 1e-06
        B, L, S = (4, 256, 256)

        def _gqa_forward(hidden_state, encoder_hidden_state, encoder_attention_mask, Wq, bq, Wk, bk, Wv, bv, Wo, bo, gamma, beta):
            b, l, _ = hidden_state.shape
            s = encoder_hidden_state.shape[1]
            q = hidden_state @ Wq + bq
            k = encoder_hidden_state @ Wk + bk
            v = encoder_hidden_state @ Wv + bv
            q = q.reshape(b, l, KVH, GROUPS, HD).transpose(0, 2, 3, 1, 4)
            k = k.reshape(b, s, KVH, HD).transpose(0, 2, 1, 3)
            v = v.reshape(b, s, KVH, HD).transpose(0, 2, 1, 3)
            scale = 1.0 / jnp.sqrt(jnp.asarray(HD, q.dtype))
            scores = jnp.einsum('bkgld,bksd->bkgls', q, k) * scale
            scores = scores + encoder_attention_mask[:, :, None, :, :]
            attn = jax.nn.softmax(scores, axis=-1)
            out = jnp.einsum('bkgls,bksd->bkgld', attn, v)
            out = out.transpose(0, 3, 1, 2, 4).reshape(b, l, H)
            out = out @ Wo + bo
            x = out + hidden_state
            mu = jnp.mean(x, axis=-1, keepdims=True)
            var = jnp.var(x, axis=-1, keepdims=True)
            return (x - mu) * jax.lax.rsqrt(var + EPS) * gamma + beta
        key = jax.random.key(seed)
        ks = jax.random.split(key, 12)
        sd = 0.02
        return {'hidden_state': jax.random.normal(ks[0], (B, L, H), jnp.float32), 'encoder_hidden_state': jax.random.normal(ks[1], (B, S, H), jnp.float32), 'encoder_attention_mask': jnp.zeros((B, 1, L, S), jnp.float32), 'Wq': jax.random.normal(ks[2], (H, H), jnp.float32) * sd, 'bq': jnp.zeros((H,), jnp.float32), 'Wk': jax.random.normal(ks[3], (H, KVH * HD), jnp.float32) * sd, 'bk': jnp.zeros((KVH * HD,), jnp.float32), 'Wv': jax.random.normal(ks[4], (H, KVH * HD), jnp.float32) * sd, 'bv': jnp.zeros((KVH * HD,), jnp.float32), 'Wo': jax.random.normal(ks[5], (H, H), jnp.float32) * sd, 'bo': jnp.zeros((H,), jnp.float32), 'gamma': jnp.ones((H,), jnp.float32), 'beta': jnp.zeros((H,), jnp.float32)}
    _L1_xattn_all = _L1_xattn_setup()
    _L1_xattn_in = {k: v for k, v in _L1_xattn_all.items() if k in ('Wq', 'bq', 'Wk', 'bk', 'Wv', 'bv', 'Wo', 'bo', 'gamma', 'beta')}
    del _L1_xattn_all
    return {'x': x, 'ctx_2048': ctx_2048, 'mask_BxS2_ik0': mask_BxS2_ik0, 'mask_Bx1xSxS2_ff0': mask_Bx1xSxS2_ff0, 'L0_xattn_q_w': _L0_xattn_in['q_w'], 'L0_xattn_q_b': _L0_xattn_in['q_b'], 'L0_xattn_kv_w': _L0_xattn_in['kv_w'], 'L0_xattn_kv_b': _L0_xattn_in['kv_b'], 'L0_xattn_out_w': _L0_xattn_in['out_w'], 'L0_xattn_out_b': _L0_xattn_in['out_b'], 'L0_xattn_postnorm_w': _L0_xattn_in['postnorm_w'], 'L0_xattn_mlp_w1': _L0_xattn_in['mlp_w1'], 'L0_xattn_mlp_b1': _L0_xattn_in['mlp_b1'], 'L0_xattn_mlp_w2': _L0_xattn_in['mlp_w2'], 'L0_xattn_mlp_b2': _L0_xattn_in['mlp_b2'], 'L1_xattn_Wq': _L1_xattn_in['Wq'], 'L1_xattn_bq': _L1_xattn_in['bq'], 'L1_xattn_Wk': _L1_xattn_in['Wk'], 'L1_xattn_bk': _L1_xattn_in['bk'], 'L1_xattn_Wv': _L1_xattn_in['Wv'], 'L1_xattn_bv': _L1_xattn_in['bv'], 'L1_xattn_Wo': _L1_xattn_in['Wo'], 'L1_xattn_bo': _L1_xattn_in['bo'], 'L1_xattn_gamma': _L1_xattn_in['gamma'], 'L1_xattn_beta': _L1_xattn_in['beta']}

def reference(x, ctx_2048, mask_BxS2_ik0, mask_Bx1xSxS2_ff0, L0_xattn_q_w, L0_xattn_q_b, L0_xattn_kv_w, L0_xattn_kv_b, L0_xattn_out_w, L0_xattn_out_b, L0_xattn_postnorm_w, L0_xattn_mlp_w1, L0_xattn_mlp_b1, L0_xattn_mlp_w2, L0_xattn_mlp_b2, L1_xattn_Wq, L1_xattn_bq, L1_xattn_Wk, L1_xattn_bk, L1_xattn_Wv, L1_xattn_bv, L1_xattn_Wo, L1_xattn_bo, L1_xattn_gamma, L1_xattn_beta):
    import jax
    import jax.numpy as jnp

    def _L0_xattn_ref(x, latents, attention_mask, q_w, q_b, kv_w, kv_b, out_w, out_b, postnorm_w, mlp_w1, mlp_b1, mlp_w2, mlp_b2):
        import jax, jax.numpy as jnp
        import numpy as np
        B, P, K, H, NH = (4, 512, 64, 512, 16)
        DH = H // NH
        EPS = 1e-06

        def rmsnorm(x, w):
            var = jnp.mean(jnp.square(x), axis=-1, keepdims=True)
            return x * jax.lax.rsqrt(var + EPS) * w
        b, p, _ = x.shape
        k_len = latents.shape[1]
        residual = latents
        h = jnp.concatenate([x, latents], axis=1)
        q = (latents @ q_w + q_b).reshape(b, k_len, NH, DH)
        kv = (h @ kv_w + kv_b).reshape(b, p + k_len, NH, DH, 2)
        kmat, v = (kv[..., 0], kv[..., 1])
        attn = jnp.einsum('bkhd,bnhd->bhkn', q, kmat) / DH
        full_mask = jnp.concatenate([attention_mask.astype(bool), jnp.ones((b, k_len), bool)], axis=-1)
        attn = jnp.where(full_mask[:, None, None, :], attn, -jnp.inf)
        attn = jax.nn.softmax(attn.astype(jnp.float32), axis=-1).astype(q.dtype)
        attn_out = jnp.einsum('bhkn,bnhd->bkhd', attn, v).reshape(b, k_len, H)
        attn_out = attn_out @ out_w + out_b + residual
        out = rmsnorm(attn_out, postnorm_w)
        out = jax.nn.gelu(out @ mlp_w1 + mlp_b1) @ mlp_w2 + mlp_b2
        return out + residual

    def _L1_xattn_ref(hidden_state, encoder_hidden_state, encoder_attention_mask, Wq, bq, Wk, bk, Wv, bv, Wo, bo, gamma, beta):
        import jax, jax.numpy as jnp
        import numpy as np
        H = 512
        NH = 32
        KVH = 8
        HD = H // NH
        GROUPS = NH // KVH
        EPS = 1e-06
        B, L, S = (4, 256, 256)

        def _gqa_forward(hidden_state, encoder_hidden_state, encoder_attention_mask, Wq, bq, Wk, bk, Wv, bv, Wo, bo, gamma, beta):
            b, l, _ = hidden_state.shape
            s = encoder_hidden_state.shape[1]
            q = hidden_state @ Wq + bq
            k = encoder_hidden_state @ Wk + bk
            v = encoder_hidden_state @ Wv + bv
            q = q.reshape(b, l, KVH, GROUPS, HD).transpose(0, 2, 3, 1, 4)
            k = k.reshape(b, s, KVH, HD).transpose(0, 2, 1, 3)
            v = v.reshape(b, s, KVH, HD).transpose(0, 2, 1, 3)
            scale = 1.0 / jnp.sqrt(jnp.asarray(HD, q.dtype))
            scores = jnp.einsum('bkgld,bksd->bkgls', q, k) * scale
            scores = scores + encoder_attention_mask[:, :, None, :, :]
            attn = jax.nn.softmax(scores, axis=-1)
            out = jnp.einsum('bkgls,bksd->bkgld', attn, v)
            out = out.transpose(0, 3, 1, 2, 4).reshape(b, l, H)
            out = out @ Wo + bo
            x = out + hidden_state
            mu = jnp.mean(x, axis=-1, keepdims=True)
            var = jnp.var(x, axis=-1, keepdims=True)
            return (x - mu) * jax.lax.rsqrt(var + EPS) * gamma + beta
        return _gqa_forward(hidden_state, encoder_hidden_state, encoder_attention_mask, Wq, bq, Wk, bk, Wv, bv, Wo, bo, gamma, beta)
    x = _L0_xattn_ref(ctx_2048, x, mask_BxS2_ik0, L0_xattn_q_w, L0_xattn_q_b, L0_xattn_kv_w, L0_xattn_kv_b, L0_xattn_out_w, L0_xattn_out_b, L0_xattn_postnorm_w, L0_xattn_mlp_w1, L0_xattn_mlp_b1, L0_xattn_mlp_w2, L0_xattn_mlp_b2)
    x = _L1_xattn_ref(x, ctx_2048, mask_Bx1xSxS2_ff0, L1_xattn_Wq, L1_xattn_bq, L1_xattn_Wk, L1_xattn_bk, L1_xattn_Wv, L1_xattn_bv, L1_xattn_Wo, L1_xattn_bo, L1_xattn_gamma, L1_xattn_beta)
    return x

_drawn_inputs = setup_inputs


def setup_inputs(seed=0):
    import zlib

    import numpy as np

    out = dict(_drawn_inputs(seed))
    spreads = {'L0_xattn_q_b': (0.0, 0.8),
     'L0_xattn_kv_b': (0.0, 0.774),
     'L0_xattn_out_b': (0.0, 1.228),
     'L0_xattn_postnorm_w': (1.0, 0.2),
     'L0_xattn_mlp_b1': (0.0, 0.1),
     'L0_xattn_mlp_b2': (0.0, 0.1),
     'L1_xattn_bq': (0.0, 0.8),
     'L1_xattn_bk': (0.0, 2.0),
     'L1_xattn_bv': (0.0, 0.1),
     'L1_xattn_bo': (0.0, 0.1),
     'L1_xattn_gamma': (1.0, 0.2),
     'L1_xattn_beta': (0.0, 0.1)}
    factors = {'L0_xattn_q_w': 8.0,
     'L0_xattn_kv_w': 8.0,
     'L0_xattn_out_w': 4.96,
     'L1_xattn_Wq': 7.34,
     'L1_xattn_Wk': 7.172}
    for name, (base, spread) in spreads.items():
        noise = np.random.default_rng([zlib.crc32(name.encode()), seed]).standard_normal(out[name].shape)
        drawn = base * np.exp(spread * noise) if base else spread * noise
        out[name] = jnp.asarray(drawn.astype(out[name].dtype))
    for name, factor in factors.items():
        out[name] = (out[name] * factor).astype(out[name].dtype)
    return out
```

```python
from contextlib import ExitStack

import concourse.bass as bass
from concourse import mybir

F32 = mybir.dt.float32
F32R = mybir.dt.float32r
I32 = mybir.dt.int32
ALU = mybir.AluOpType
ACT = mybir.ActivationFunctionType
AX = mybir.AxisListType

B, R, H = 16, 128, 512
P = 128
KC = H // P
FF = 4 * H
FC = FF // P
EPS = 1e-6
HEADS0, DH0 = 16, 32
HEADS1, KV1, DH1 = 32, 8, 16
GROUPS1 = HEADS1 // KV1
NEWTON = 3
NEG = -1e30
SB = 4
RC = 2
ROUNDS = KC // RC
HALVES = ("hi", "lo")
PASSES = ((0, 0), (0, 1), (1, 0))


class Walk:

    def __init__(self, per_step):
        self.per_step, self.n, self.it, self.steps = per_step, dict.fromkeys(per_step, 0), None, 0

    def enter(self, it, steps):
        self.it, self.steps, self.entered = it, steps, dict(self.n)

    def leave(self, iterations):
        for name, per in self.per_step.items():
            assert self.n[name] in (self.entered[name], self.entered[name] + per * self.steps), name
            if self.n[name] != self.entered[name]:
                self.n[name] += per * self.steps * (iterations - 1)
        self.it = None

    def so_far(self, name, slots=1, slot=0):
        before = (self.n[name] - slot + slots - 1) // slots
        if self.it is not None:
            assert self.per_step[name] * self.steps % slots == 0
            before = before + self.it * (self.per_step[name] * self.steps // slots)
        return before

    def use(self, name, slots=1):
        slot = self.n[name] % slots
        before = self.so_far(name, slots, slot)
        self.n[name] += 1
        return slot, before

    def event(self, name):
        return self.use(name)[1] + 1


def by_chunk(weight):
    return weight.rearrange("(k p) n -> p k n", p=P)


def split_product(nc, out, stationary, moving, chunks, first=True, last=True):
    for k in range(chunks):
        for a, b in PASSES:
            mm = nc.tensor.matmul(out, stationary(a, k), moving(b, k),
                                  start=first and k == 0 and (a, b) == PASSES[0],
                                  stop=last and k == chunks - 1 and (a, b) == PASSES[-1])
    return mm


def xattn_kernel(nc, x, ctx_rows, key_mask, add_mask, q_w0, q_b0, kv_w0, kv_b0, out_w0, out_b0, post_w0,
                 w1, b1, w2, b2, Wq, bq, Wk, bk, Wv, bv, Wo, bo, gamma, beta, out):
    with ExitStack() as top:
        ident = top.enter_context(nc.sbuf_tensor("ident", [P, P], F32))
        between = top.enter_context(nc.sbuf_tensor("between", [P, KC, B * R], F32))
        S = [top.enter_context(nc.psum_tensor(f"S{j}", [P, 512], F32)) for j in range(SB)]
        J = [top.enter_context(nc.psum_tensor(f"J{j}", [P, 512], F32)) for j in range(2)]
        O = top.enter_context(nc.psum_tensor("O", [P, 512], F32))
        T = top.enter_context(nc.psum_tensor("T", [P, 512], F32))
        banks = (S, J, O, T)
        attention(nc, top, 0, ident, between, banks, x, ctx_rows, key_mask, q_w0, q_b0,
                  (kv_w0, kv_b0), out_w0, out_b0, post_w0, None, None)
        mlp(nc, top, between, S, J, x, w1, b1, w2, b2)
        attention(nc, top, 1, ident, between, banks, x, ctx_rows, add_mask, Wq, bq,
                  (Wk, bk, Wv, bv), Wo, bo, gamma, beta, out)


def attention(nc, top, L, ident, between, banks, x, ctx_rows, mask, q_w, q_b, kv, o_w, o_b,
              norm_w, norm_b, out):
    S, J, O, T = banks
    st = ExitStack()

    def sb(name, shape, dt=F32):
        return st.enter_context(nc.sbuf_tensor(f"{name}_{L}", shape, dt))

    def sem(name):
        return top.enter_context(nc.semaphore(f"{name}_{L}"))

    keys = 2 * R if L == 0 else R
    per_bank = 512 // keys
    scale = 1.0 / DH0 if L == 0 else float(DH1) ** -0.5
    KW = H if L == 0 else KV1 * DH1
    with st:
        wq = [sb(f"wq{h}", [P, KC, H], F32R) for h in HALVES]
        wo = [sb(f"wo{h}", [P, KC, H], F32R) for h in HALVES]
        if L == 0:
            wk = [sb(f"wk{h}", [P, KC, KW], F32R) for h in HALVES]
            wv = [sb(f"wv{h}", [P, KC, KW], F32R) for h in HALVES]
        else:
            wkv = [sb(f"wkv{h}", [P, KC, 2 * KW], F32R) for h in HALVES]
        stage = [sb(f"stage{i}", [P, KC * H]) for i in range(2)]
        bq_all = sb("bq_all", [P, H])
        bo_all = sb("bo_all", [P, H])
        nw_all = sb("nw_all", [P, H])
        bkv_all = sb("bkv_all", [P, 2 * KW])
        if L == 0:
            bk_part = sb("bk_part", [P, KC, 2])
        else:
            nb_all = sb("nb_all", [P, H])
            parity = sb("parity", [P, 2])
        rows = [sb(f"rows{i}", [P, 2, H]) for i in range(2)]
        resid = [sb(f"resid{i}", [P, H]) for i in range(2)]
        hT = [sb(f"hT{h}", [P, KC, 2, R], F32R) for h in HALVES]
        Qn = sb("Qn", [P, H])
        QT = [sb(f"QT{i}", [P, KC, R]) for i in range(2)]
        if L == 0:
            KT = [sb(f"KT{i}", [P, KC, keys]) for i in range(2)]
            V = [sb(f"V{i}", [P, 2, H]) for i in range(2)]
            mrow = [sb(f"mrow{i}", [P, R], I32) for i in range(2)]
            madd = [sb(f"madd{i}", [P, keys]) for i in range(2)]
        else:
            Kn = sb("Kn", [P, KW])
            KT = [sb(f"KT{i}", [P, 2, R]) for i in range(2)]
            V = [sb(f"V{i}", [P, SB, 2, 32]) for i in range(2)]
            madd = [sb(f"madd{i}", [P, R]) for i in range(2)]
        pr = [sb(f"pr{i}", [P, SB, 512]) for i in range(2)]
        nmax = [sb(f"nmax{i}", [P, SB * per_bank]) for i in range(2)]
        den = [sb(f"den{i}", [P, SB * per_bank]) for i in range(2)]
        rec = [sb(f"rec{i}", [P, RC, P]) for i in range(2)]
        pT = sb("pT", [P, SB, 512])
        recT = sb("recT", [P, RC, R])
        aT = sb("aT", [P, RC, R])
        aTs = [sb(f"aT{h}", [P, KC, R], F32R) for h in HALVES]
        res = sb("res", [P, H])
        nrm = sb("nrm", [P, H])
        stat = sb("stat", [P, 16])
        if L == 0:
            squares = sb("squares", [P, H])
        else:
            fin = [sb(f"fin{i}", [P, H]) for i in range(2)]

        stage_loaded = [sem(f"stage_loaded{i}") for i in range(2)]
        w_hi, w_split, consts_loaded, zeroed, prepared = map(
            sem, ("w_hi", "w_split", "consts_loaded", "zeroed", "prepared"))
        rows_loaded = [sem(f"rows_loaded{i}") for i in range(2)]
        mask_loaded = [sem(f"mask_loaded{i}") for i in range(2)]
        stored = [sem(f"stored{i}") for i in range(2)]
        J_full = [sem(f"J_full{i}") for i in range(2)]
        J_taken = [sem(f"J_taken{i}") for i in range(2)]
        S_full = [sem(f"S_full{i}") for i in range(SB)]
        S_taken = [sem(f"S_taken{i}") for i in range(SB)]
        O_full, O_taken, T_full, T_taken = map(sem, ("O_full", "O_taken", "T_full", "T_taken"))
        (resid_ready, madd_ready, hT_hi, max_ready, p_ready, rec_ready, aT_hi, aT_lo, squared,
         small, nrm_ready, scaled, fin_ready) = map(
            sem, ("resid_ready", "madd_ready", "hT_hi", "max_ready", "p_ready", "rec_ready", "aT_hi",
                  "aT_lo", "squared", "small", "nrm_ready", "scaled", "fin_ready"))

        PER_STEP = dict(J=8 if L == 0 else 3, S=2 * ROUNDS, O=ROUNDS, T=2 + 1 + 1 + ROUNDS,
                        entry=1, hT=2, round=ROUNDS, bank=SB * ROUNDS, aT=ROUNDS, done=1,
                        small=(1 if L == 0 else 4) + 2 + 2 * NEWTON)
        ROW_LOADS = 2 if L == 0 else 3
        CONSTS = 16 * (5 if L == 0 else 6)
        PREPARED = 1 if L == 0 else 2

        def project(do, b, s):
            do["turn"](b, s)
            do["query"](b, s)
            for t in range(KC if L == 0 else 1):
                do["key"](b, s, t)
            do["turn_query"](b, s)
            if L == 0:
                do["value"](b, s, 0)
                do["value"](b, s, 1)
            else:
                do["turn_key"](b, s)

        def step(do, b, s, ahead=True, behind=True):
            o = 1 - s
            do["scores"](b, s, 0)
            if behind:
                do["output"](b - 1, o)
            if ahead:
                do["turn"](b + 1, o)
            do["probs"](b, s, 0)
            if ahead:
                do["query"](b + 1, o)
                do["key"](b + 1, o, 0)
            if behind:
                do["finish"](b - 1, o)
            do["values"](b, s, 0)
            do["scores"](b, s, 1)
            if ahead:
                if L == 0:
                    do["key"](b + 1, o, 1)
                do["turn_query"](b + 1, o)
                if L == 0:
                    do["key"](b + 1, o, 2)
                    do["value"](b + 1, o, 0)
                else:
                    do["turn_key"](b + 1, o)
            do["probs"](b, s, 1)
            if ahead and L == 0:
                do["key"](b + 1, o, 3)
                do["value"](b + 1, o, 1)
            do["values"](b, s, 1)

        def all_steps(eng, w, do):
            project(do, 0, 0)
            step(do, 0, 0, behind=False)
            with eng.Fori(0, (B - 2) // 2) as it:
                w.enter(it, 2)
                step(do, it * 2 + 1, 1)
                step(do, it * 2 + 2, 0)
                w.leave((B - 2) // 2)
            step(do, B - 1, 1, ahead=False)
            do["output"](B - 1, 1)
            do["finish"](B - 1, 1)

        def staged(u, n):
            return stage[u % 2][:, :].rearrange("p (k n) -> p k n", n=n)

        units = [([(staged(0, H), by_chunk(q_w))], [(staged(0, H), wq)])]
        if L == 0:
            for u in range(2):
                ks = slice(2 * u, 2 * u + 2)
                pairs = staged(u + 1, 2 * KW).rearrange("p k (f two) -> p k f two", two=2)
                units.append(([(staged(u + 1, 2 * KW), by_chunk(kv[0])[:, ks, :])],
                              [(pairs[:, :, :, n], [w_[:, ks, :] for w_ in ww])
                               for n, ww in enumerate((wk, wv))]))
            units.append(([(staged(3, H), by_chunk(o_w))], [(staged(3, H), wo)]))
        else:
            kv_st = stage[1][:, 0:KC * 2 * KW].rearrange("p (k n) -> p k n", k=KC)
            units.append(([(kv_st[:, :, 0:KW], by_chunk(kv[0])), (kv_st[:, :, KW:2 * KW], by_chunk(kv[2]))],
                          [(kv_st, wkv)]))
            o_rows = o_w.rearrange("(g c d) n -> g d c n", c=GROUPS1, d=DH1)
            units.append(([(staged(2, H)[DH1 * g:DH1 * (g + 1)], o_rows[g]) for g in range(KV1)],
                          [(staged(2, H), wo)]))
        splits_before = [sum(len(s) for _, s in units[:u]) for u in range(len(units) + 1)]
        loads_to_slot = [sum(len(units[v][0]) for v in range(u % 2, u + 1, 2)) for u in range(len(units))]

        with nc.Block() as block:

            @block.sync
            def _(sp):
                def load_rows(b, s):
                    sp.dma_start(rows[s][:, 0, :], ctx_rows[b]).then_inc(rows_loaded[s], 16)
                    if L == 0:
                        sp.dma_start(rows[s][:, 1, :], x[b]).then_inc(rows_loaded[s], 16)
                    else:
                        for a in range(2):
                            sp.dma_start(rows[s][:, 1, a * 256:(a + 1) * 256],
                                         between[:, 2 * s + a, bass.ds((b - s) * R, 256)])\
                                .then_inc(rows_loaded[s], 16)

                def load_mask(b, s):
                    if L == 0:
                        sp.dma_start(mrow[s][:, :], mask[b].partition_broadcast(P)).then_inc(mask_loaded[s], 16)
                    else:
                        sp.dma_start(madd[s][:, :], mask[b, 0]).then_inc(mask_loaded[s], 16)

                def load_next(b, s):
                    entries, halves = b + 1, b * 2 + 2
                    if not isinstance(b, int):
                        entries, halves = sp.snap(entries), sp.snap(halves)
                    sp.wait_ge(resid_ready, entries)
                    sp.wait_ge(hT_hi, halves)
                    load_rows(b + 2, s)
                    if L == 0:
                        sp.wait_ge(madd_ready, b + 1)
                    else:
                        sp.wait_ge(max_ready, (b + 1) * (SB * ROUNDS))
                    load_mask(b + 2, s)

                def store(b, s):
                    if L == 1:
                        sp.wait_ge(fin_ready, b + 1)
                        sp.dma_start(out[b], fin[s][:, :]).then_inc(stored[s], 16)

                if L == 1:
                    for s in range(2):
                        sp.nop().then_inc(stored[s], 16)
                load_rows(0, 0)
                for u, (loads, _) in enumerate(units):
                    if u >= 2:
                        sp.wait_ge(w_split, splits_before[u - 1])
                    for to, frm in loads:
                        sp.dma_start(to, frm).then_inc(stage_loaded[u % 2], 16)
                load_mask(0, 0)
                load_rows(1, 1)
                load_mask(1, 1)
                load_next(0, 0)
                with sp.Fori(0, (B - 4) // 2) as it:
                    load_next(it * 2 + 1, 1)
                    store(it * 2, 0)
                    load_next(it * 2 + 2, 0)
                    store(it * 2 + 1, 1)
                load_next(B - 3, 1)
                for b in range(B - 4, B):
                    store(b, b % 2)
                if L == 1:
                    for s in range(2):
                        sp.wait_ge(stored[s], 16 * (B // 2 + 1))

            @block.gpsimd
            def _(pool):
                vectors = [(bq_all[:, :], q_b), (bo_all[:, :], o_b), (nw_all[:, :], norm_w)]
                if L == 0:
                    vectors += [(bkv_all[:, :], kv[1])]
                else:
                    vectors += [(bkv_all[:, 0:KW], kv[1]), (bkv_all[:, KW:2 * KW], kv[3]),
                                (nb_all[:, :], norm_b)]
                for to, frm in vectors:
                    pool.dma_start(to, frm.partition_broadcast(P)).then_inc(consts_loaded, 16)
                if L == 0:
                    pool.dma_start(bk_part[:, :, :], kv[1].rearrange("(c p two) -> p c two", p=P, two=2))\
                        .then_inc(consts_loaded, 16)
                    pool.memset(ident[:, :], 0.0).then_inc(zeroed, 1)
                    for s in range(2):
                        pool.memset(madd[s][:, R:2 * R], 0.0).then_inc(zeroed, 1)
                    pool.wait_ge(zeroed, 3)
                    pool.affine_select(out=ident[:, :], in_=ident[:, :], compare_op=ALU.not_equal,
                                       fill=1.0, base=0, pattern=[[-1, P]], channel_multiplier=1)\
                        .then_inc(prepared, 1)
                else:
                    for s in range(2):
                        pool.memset(V[s][:, :, :, :], 0.0).then_inc(prepared, 1)
                pool.wait_ge(consts_loaded, CONSTS)

                def residual(b, s, uses):
                    if not isinstance(b, int):
                        pool.wait_ge(nrm_ready, b - 1)
                    pool.wait_ge(rows_loaded[s], (uses + 1) * (16 * ROW_LOADS))
                    pool.tensor_tensor(resid[s][:, :], rows[s][:, 1, :], bo_all[:, :], ALU.add)\
                        .then_inc(resid_ready, 1)

                def scale_and_shift(b, s, uses):
                    if L == 1:
                        pool.wait_ge(nrm_ready, b + 1)
                        pool.wait_ge(stored[s], uses * 16 + 16)
                        pool.tensor_tensor(fin[s][:, :], nrm[:, :], nw_all[:, :], ALU.mult).then_inc(scaled, 1)
                        pool.wait_ge(scaled, b + 2)
                        pool.tensor_tensor(fin[s][:, :], fin[s][:, :], nb_all[:, :], ALU.add)\
                            .then_inc(fin_ready, 1)

                if L == 1:
                    pool.nop().then_inc(scaled, 1)
                residual(0, 0, 0)
                residual(1, 1, 0)
                with pool.Fori(0, (B - 2) // 2) as it:
                    for s in range(2):
                        residual(it * 2 + s + 2, s, it + 1)
                        scale_and_shift(it * 2 + s, s, it)
                for s in range(2):
                    scale_and_shift(B - 2 + s, s, (B - 2) // 2)

            @block.scalar
            def _(act):
                w = Walk(PER_STEP)
                for u, (_, splits) in enumerate(units):
                    act.wait_ge(stage_loaded[u % 2], 16 * loads_to_slot[u])
                    for frm, (hi, _) in splits:
                        nc.scalar.activation(hi[:, :, :], frm, ACT.Copy).then_inc(w_hi, 1)
                act.wait_ge(consts_loaded, CONSTS)
                act.wait_ge(prepared, PREPARED)

                def turn(b, s):
                    for kind in range(2):
                        _, n = w.use("T")
                        act.wait_ge(T_full, n + 1)
                        nc.scalar.activation(hT[0][:, :, kind, :], T[:, :].rearrange("p (k r) -> p k r", k=KC),
                                             ACT.Copy).then_inc(hT_hi, 1)

                def query(b, s):
                    w.use("J")

                def key(b, s, c):
                    j, n = w.use("J", 2)
                    if L == 0:
                        act.wait_ge(J_full[j], n + 1)
                        nc.scalar.activation(KT[s][:, c, :], J[j][:, 0:keys], ACT.Identity,
                                             bias=bk_part[:, c, 0:1]).then_inc(J_taken[j], 1)

                def value(b, s, kind):
                    w.use("J")

                def turn_query(b, s):
                    _, n = w.use("T")
                    act.wait_ge(T_full, n + 1)
                    nc.scalar.activation(QT[s][:, :, :], T[:, :].rearrange("p (k r) -> p k r", k=KC),
                                         ACT.Copy).then_inc(T_taken, 1)

                def turn_key(b, s):
                    _, n = w.use("T")
                    act.wait_ge(T_full, n + 1)
                    for a in range(2):
                        last = nc.scalar.activation(KT[s][:, a, :], T[:, 0:R], ACT.Copy,
                                                    scale=parity[:, a:a + 1])
                    last.then_inc(T_taken, 1)

                def scores(b, s, r):
                    slot, _ = w.use("round", 2)
                    w.use("S")
                    for j in range(SB):
                        n = w.event("bank")
                        act.wait_ge(max_ready, n)
                        for h in range(per_bank):
                            part = pr[slot][:, j, h * keys:(h + 1) * keys]
                            at = slice(j * per_bank + h, j * per_bank + h + 1)
                            last = nc.scalar.activation(part, part, ACT.Exp, bias=nmax[slot][:, at],
                                                        accum_out=den[slot][:, at])
                        last.then_inc(p_ready, 1)

                def probs(b, s, r):
                    _, n = w.use("S")
                    for j in range(1, SB, 2):
                        act.wait_ge(S_full[j], n + 1)
                        nc.scalar.activation(pT[:, j, :], S[j][:, :], ACT.Copy).then_inc(S_taken[j], 1)

                def values(b, s, r):
                    _, n = w.use("T")
                    act.wait_ge(T_full, n + 1)
                    nc.scalar.activation(recT[:, :, :], T[:, 0:RC * R].rearrange("p (c r) -> p c r", c=RC),
                                         ACT.Copy).then_inc(T_taken, 1)
                    _, n = w.use("O")
                    act.wait_ge(O_taken, n + 1)
                    nc.scalar.activation(aTs[0][:, RC * r:RC * (r + 1), :], aT[:, :, :], ACT.Copy)\
                        .then_inc(aT_hi, 1)

                def output(b, s):
                    j, n = w.use("J", 2)
                    if L == 0:
                        act.wait_ge(J_taken[j], n + 1)
                        nc.scalar.activation(squares[:, :], res[:, :], ACT.Square, accum_out=stat[:, 0:1])\
                            .then_inc(squared, 1)

                def finish(b, s):
                    if L == 0:
                        _, n = w.use("T")
                        act.wait_ge(T_full, n + 1)
                        nc.scalar.activation(between[:, :, bass.ds(b * R, R)],
                                             T[:, :].rearrange("p (k r) -> p k r", k=KC),
                                             ACT.Copy).then_inc(T_taken, 1)

                all_steps(act, w, dict(turn=turn, query=query, key=key, value=value, turn_query=turn_query,
                                       turn_key=turn_key, scores=scores, probs=probs, values=values,
                                       output=output, finish=finish))

            @block.vector
            def _(dve):
                w = Walk(PER_STEP)
                if L == 1:
                    dve.wait_ge(prepared, PREPARED)
                    halves = ident[:, :].rearrange("p (m a d) -> p a m d", a=2, d=DH1)
                    for a in range(2):
                        last = nc.vector.tensor_reduce(parity[:, a:a + 1], halves[:, a], AX.XY, ALU.add)
                    last.then_inc(zeroed, 1)
                for u, (_, splits) in enumerate(units):
                    for v, (frm, (hi, lo)) in enumerate(splits):
                        dve.wait_ge(w_hi, splits_before[u] + v + 1)
                        nc.vector.tensor_tensor(lo[:, :, :], frm, hi[:, :, :].bitcast(F32), ALU.subtract)\
                            .then_inc(w_split, 1)
                dve.wait_ge(consts_loaded, CONSTS)
                dve.wait_ge(prepared, PREPARED)

                def turn(b, s):
                    if L == 0:
                        _, n = w.use("entry", 2)
                        dve.wait_ge(mask_loaded[s], (n + 1) * 16)
                        nc.vector.tensor_scalar(madd[s][:, 0:R], mrow[s][:, :], 0.0, NEG, ALU.is_equal,
                                                ALU.mult).then_inc(madd_ready, 1)
                    for kind in range(2):
                        _, n = w.use("T")
                        dve.wait_ge(T_full, n + 1)
                        dve.wait_ge(hT_hi, w.event("hT"))
                        nc.vector.tensor_tensor(hT[1][:, :, kind, :], T[:, :].rearrange("p (k r) -> p k r", k=KC),
                                                hT[0][:, :, kind, :].bitcast(F32), ALU.subtract)\
                            .then_inc(T_taken, 1)

                def query(b, s):
                    j, n = w.use("J", 2)
                    dve.wait_ge(J_full[j], n + 1)
                    if L == 0:
                        nc.vector.tensor_tensor(Qn[:, :], J[j][:, :], bq_all[:, :], ALU.add)\
                            .then_inc(J_taken[j], 1)
                    else:
                        def by_group(t):
                            return t[:, :].rearrange("p (g c d) -> p g c d", c=GROUPS1, d=DH1)
                        nc.vector.tensor_tensor(Qn[:, :].rearrange("p (c g d) -> p g c d", c=GROUPS1, d=DH1),
                                                by_group(J[j]), by_group(bq_all), ALU.add)\
                            .then_inc(J_taken[j], 1)

                def key(b, s, c):
                    j, n = w.use("J", 2)
                    if L == 1:
                        dve.wait_ge(J_full[j], n + 1)
                        nc.vector.tensor_tensor(Kn[:, :], J[j][:, 0:KW], bkv_all[:, 0:KW], ALU.add)
                        for a in range(2):
                            def heads(t):
                                return t[:, KW:2 * KW].rearrange("p (m a d) -> p a m d", a=2, d=DH1)[:, a]
                            last = nc.vector.tensor_tensor(V[s][:, :, a, a * DH1:(a + 1) * DH1],
                                                           heads(J[j]), heads(bkv_all), ALU.add)
                        last.then_inc(J_taken[j], 1)

                def value(b, s, kind):
                    j, n = w.use("J", 2)
                    dve.wait_ge(J_full[j], n + 1)
                    nc.vector.tensor_tensor(V[s][:, kind, :], J[j][:, :],
                                            bkv_all[:, :].rearrange("p (f two) -> p f two", two=2)[:, :, 1],
                                            ALU.add).then_inc(J_taken[j], 1)

                def turn_query(b, s):
                    w.use("T")

                def turn_key(b, s):
                    w.use("T")

                def scores(b, s, r):
                    slot, _ = w.use("round", 2)
                    _, n = w.use("S")
                    if r == 0:
                        if L == 0:
                            dve.wait_ge(madd_ready, b + 1)
                        else:
                            _, m = w.use("entry", 2)
                            dve.wait_ge(mask_loaded[s], (m + 1) * 16)
                    for j in range(SB):
                        w.event("bank")
                        part = pr[slot][:, j, :].rearrange("p (h k) -> p h k", k=keys)
                        dve.wait_ge(S_full[j], n + 1)
                        nc.vector.scalar_tensor_tensor(
                            part, S[j][:, :].rearrange("p (h k) -> p h k", k=keys), scale,
                            madd[s][:, :].unsqueeze(1).broadcast_to([P, per_bank, keys]),
                            ALU.mult, ALU.add).then_inc(S_taken[j], 1)
                        dve.wait_ge(S_taken[j], n + 1)
                        nc.vector.tensor_reduce(nmax[slot][:, j * per_bank:(j + 1) * per_bank], part,
                                                AX.X, ALU.max, negate=True).then_inc(max_ready, 1)

                def probs(b, s, r):
                    slot = r % 2
                    _, n = w.use("S")
                    dve.wait_ge(p_ready, w.so_far("bank"))
                    for c in range(RC):
                        if L == 0:
                            heads = den[slot][:, :].rearrange("p (j c) -> p c j", c=RC)[:, c]
                            spread = heads.unsqueeze(2).broadcast_to([P, SB, DH0])
                            to = rec[slot][:, c, :].rearrange("p (j d) -> p j d", j=SB)
                        else:
                            heads = den[slot][:, :].rearrange("p (j c a) -> p c j a", c=RC, a=2)[:, c]
                            spread = heads.unsqueeze(3).broadcast_to([P, SB, 2, DH1])
                            to = rec[slot][:, c, :].rearrange("p (j a d) -> p j a d", j=SB, a=2)
                        last = nc.vector.reciprocal(to, spread)
                    last.then_inc(rec_ready, 1)
                    for j in range(0, SB, 2):
                        dve.wait_ge(S_full[j], n + 1)
                        nc.vector.tensor_copy(pT[:, j, :], S[j][:, :]).then_inc(S_taken[j], 1)

                def values(b, s, r):
                    _, t = w.use("T")
                    _, n = w.use("O")
                    dve.wait_ge(T_taken, t + 1)
                    dve.wait_ge(O_full, n + 1)
                    nc.vector.tensor_tensor(aT[:, :, :], O[:, 0:RC * R].rearrange("p (c r) -> p c r", c=RC),
                                            recT[:, :, :], ALU.mult).then_inc(O_taken, 1)
                    dve.wait_ge(aT_hi, w.event("aT"))
                    rs = slice(RC * r, RC * (r + 1))
                    nc.vector.tensor_tensor(aTs[1][:, rs, :], aT[:, :, :], aTs[0][:, rs, :].bitcast(F32),
                                            ALU.subtract).then_inc(aT_lo, 1)

                def inverse_root():
                    m, y, t, h = (stat[:, c:c + 1] for c in (1, 2, 3, 10))
                    nc.vector.tensor_scalar(h, m, -0.5, None, ALU.mult)
                    nc.vector.tensor_scalar(t.bitcast(I32), m.bitcast(I32), 1, None, ALU.logical_shift_right)\
                        .then_inc(small, 1)
                    dve.wait_ge(small, w.event("small"))
                    nc.vector.tensor_scalar(y.bitcast(I32), t.bitcast(I32), -1.0, float(0x5F3759DF), ALU.mult,
                                            ALU.add).then_inc(small, 1)
                    dve.wait_ge(small, w.event("small"))
                    for _ in range(NEWTON):
                        nc.vector.scalar_tensor_tensor(t, y, h, y, ALU.mult, ALU.mult).then_inc(small, 1)
                        dve.wait_ge(small, w.event("small"))
                        nc.vector.scalar_tensor_tensor(y, t, 1.5, y, ALU.add, ALU.mult).then_inc(small, 1)
                        dve.wait_ge(small, w.event("small"))

                def output(b, s):
                    j, n = w.use("J", 2)
                    done = w.event("done")
                    dve.wait_ge(resid_ready, b + 1)
                    dve.wait_ge(J_full[j], n + 1)
                    nc.vector.tensor_tensor(res[:, :], J[j][:, :], resid[s][:, :], ALU.add)\
                        .then_inc(J_taken[j], 1)
                    if L == 0:
                        dve.wait_ge(squared, done)
                        nc.vector.tensor_scalar(stat[:, 1:2], stat[:, 0:1], 1.0 / H, EPS, ALU.mult, ALU.add)\
                            .then_inc(small, 1)
                        dve.wait_ge(small, w.event("small"))
                        inverse_root()
                        nc.vector.scalar_tensor_tensor(nrm[:, :], res[:, :], stat[:, 2:3], nw_all[:, :],
                                                       ALU.mult, ALU.mult).then_inc(nrm_ready, 1)
                    else:
                        dve.wait_ge(J_taken[j], n + 1)
                        nc.vector.bn_stats(stat[:, 4:10], res[:, :]).then_inc(small, 1)
                        dve.wait_ge(small, w.event("small"))
                        mean_e, var_e, mean_o, var_o, gap, var = (
                            stat[:, c:c + 1] for c in (5, 6, 8, 9, 11, 12))
                        nc.vector.tensor_tensor(stat[:, 0:1], mean_e, mean_o, ALU.add)
                        nc.vector.scalar_tensor_tensor(var, var_e, H * EPS, var_o, ALU.add, ALU.add)
                        nc.vector.tensor_tensor(gap, mean_e, mean_o, ALU.subtract).then_inc(small, 1)
                        dve.wait_ge(small, w.event("small"))
                        nc.vector.tensor_scalar(stat[:, 0:1], stat[:, 0:1], 0.5, None, ALU.mult)
                        nc.vector.scalar_tensor_tensor(stat[:, 13:14], gap, 0.25, gap, ALU.mult, ALU.mult)\
                            .then_inc(small, 1)
                        dve.wait_ge(small, w.event("small"))
                        nc.vector.scalar_tensor_tensor(stat[:, 1:2], var, 1.0 / H, stat[:, 13:14], ALU.mult,
                                                       ALU.add).then_inc(small, 1)
                        dve.wait_ge(small, w.event("small"))
                        inverse_root()
                        dve.wait_ge(scaled, done)
                        nc.vector.tensor_scalar(nrm[:, :], res[:, :], stat[:, 0:1], stat[:, 2:3],
                                                ALU.subtract, ALU.mult).then_inc(nrm_ready, 1)

                def finish(b, s):
                    if L == 0:
                        w.use("T")

                all_steps(dve, w, dict(turn=turn, query=query, key=key, value=value, turn_query=turn_query,
                                       turn_key=turn_key, scores=scores, probs=probs, values=values,
                                       output=output, finish=finish))

            @block.tensor
            def _(pe):
                w = Walk(PER_STEP)
                pe.wait_ge(prepared, PREPARED)
                if L == 1:
                    pe.wait_ge(zeroed, 1)
                pe.wait_ge(w_split, splits_before[-1])

                def turn(b, s):
                    _, e = w.use("entry", 2)
                    pe.wait_ge(rows_loaded[s], (e + 1) * (16 * ROW_LOADS))
                    for kind in range(2):
                        _, n = w.use("T")
                        pe.wait_ge(T_taken, n)
                        for k in range(KC):
                            mm = nc.tensor.transpose(T[:, k * R:(k + 1) * R], rows[s][:, kind, k * P:(k + 1) * P],
                                                     ident[:, :])
                        mm.then_inc(T_full, 1)

                def query(b, s):
                    pe.wait_ge(T_taken, w.so_far("T"))
                    j, n = w.use("J", 2)
                    pe.wait_ge(J_taken[j], n)
                    split_product(nc, J[j][:, :], lambda h, k: hT[h][:, k, 1, :], lambda h, k: wq[h][:, k, :], KC)\
                        .then_inc(J_full[j], 1)

                def key(b, s, c):
                    j, n = w.use("J", 2)
                    pe.wait_ge(J_taken[j], n)
                    if L == 0:
                        mm = split_product(nc, J[j][:, 0:keys], lambda h, k: wk[h][:, k, c * P:(c + 1) * P],
                                           lambda h, k: hT[h][:, k, :, :], KC)
                    else:
                        mm = split_product(nc, J[j][:, 0:2 * KW], lambda h, k: hT[h][:, k, 0, :],
                                           lambda h, k: wkv[h][:, k, :], KC)
                    mm.then_inc(J_full[j], 1)

                def value(b, s, kind):
                    j, n = w.use("J", 2)
                    pe.wait_ge(J_taken[j], n)
                    split_product(nc, J[j][:, :], lambda h, k: hT[h][:, k, kind, :],
                                  lambda h, k: wv[h][:, k, :], KC).then_inc(J_full[j], 1)

                def turn_query(b, s):
                    for i in range(2):
                        pe.wait_ge(J_taken[i], w.so_far("J", 2, i))
                    _, n = w.use("T")
                    pe.wait_ge(T_taken, n)
                    for c in range(KC):
                        mm = nc.tensor.transpose(T[:, c * R:(c + 1) * R], Qn[:, c * P:(c + 1) * P], ident[:, :])
                    mm.then_inc(T_full, 1)

                def turn_key(b, s):
                    _, n = w.use("T")
                    pe.wait_ge(T_taken, n)
                    nc.tensor.transpose(T[:, 0:R], Kn[:, :], ident[:, :]).then_inc(T_full, 1)

                def scores(b, s, r):
                    if r == 0:
                        for i in range(2):
                            pe.wait_ge(J_taken[i], w.so_far("J", 2, i))
                        pe.wait_ge(T_taken, w.so_far("T"))
                    _, n = w.use("S")
                    for c in range(RC):
                        for j in range(SB):
                            if c == 0:
                                pe.wait_ge(S_taken[j], n)
                            strip = slice(32 * j, 32 * (j + 1))
                            k_ap = KT[s][strip, RC * r + c, :] if L == 0 else KT[s][strip, :, :]
                            mm = nc.tensor.matmul(S[j][:, c * 256:(c + 1) * 256], QT[s][strip, RC * r + c, :],
                                                  k_ap, start=True, stop=True)
                            if c == RC - 1:
                                mm.then_inc(S_full[j], 1)

                def probs(b, s, r):
                    slot = r % 2
                    _, n = w.use("S")
                    for j in range(SB):
                        pe.wait_ge(p_ready, w.event("bank"))
                        pe.wait_ge(S_taken[j], n)
                        for q in range(4):
                            to = q if L == 0 else (q % 2) * 2 + q // 2
                            mm = nc.tensor.transpose(S[j][:, to * P:(to + 1) * P],
                                                     pr[slot][:, j, q * P:(q + 1) * P], ident[:, :])
                        mm.then_inc(S_full[j], 1)

                def values(b, s, r):
                    slot = r % 2
                    _, n = w.use("T")
                    pe.wait_ge(T_taken, n)
                    pe.wait_ge(rec_ready, w.event("round"))
                    for c in range(RC):
                        mm = nc.tensor.transpose(T[:, c * R:(c + 1) * R], rec[slot][:, c, :], ident[:, :])
                    mm.then_inc(T_full, 1)
                    _, n = w.use("O")
                    pe.wait_ge(O_taken, n)
                    for j in range(SB):
                        pe.wait_ge(S_taken[j], w.so_far("S"))
                    if L == 0:
                        for c in range(RC):
                            for kind in range(2):
                                for j in range(SB):
                                    head = 4 * (RC * r + c) + j
                                    at = (c * 2 + kind) * R
                                    mm = nc.tensor.matmul(O[32 * j:32 * (j + 1), c * R:(c + 1) * R],
                                                          V[s][:, kind, head * DH0:(head + 1) * DH0],
                                                          pT[:, j, at:at + R], start=kind == 0, stop=kind == 1)
                    else:
                        for a in range(2):
                            for j in range(SB):
                                mm = nc.tensor.matmul(O[32 * j:32 * (j + 1), 0:RC * R], V[s][:, j, a, :],
                                                      pT[:, j, a * RC * R:(a + 1) * RC * R],
                                                      start=a == 0, stop=a == 1)
                    mm.then_inc(O_full, 1)

                def output(b, s):
                    pe.wait_ge(aT_lo, (w.event("done")) * ROUNDS)
                    j, n = w.use("J", 2)
                    pe.wait_ge(J_taken[j], n)
                    split_product(nc, J[j][:, :], lambda h, k: aTs[h][:, k, :], lambda h, k: wo[h][:, k, :], KC)\
                        .then_inc(J_full[j], 1)

                def finish(b, s):
                    if L == 0:
                        _, n = w.use("T")
                        pe.wait_ge(T_taken, n)
                        pe.wait_ge(nrm_ready, w.so_far("done"))
                        for k in range(KC):
                            mm = nc.tensor.transpose(T[:, k * R:(k + 1) * R], nrm[:, k * P:(k + 1) * P], ident[:, :])
                        mm.then_inc(T_full, 1)

                all_steps(pe, w, dict(turn=turn, query=query, key=key, value=value, turn_query=turn_query,
                                      turn_key=turn_key, scores=scores, probs=probs, values=values,
                                      output=output, finish=finish))


def mlp(nc, top, between, S, J, x, w1, b1, w2, b2):
    PAIRS, PR = B // 2, 2 * R
    LAG = 2
    RING = 4
    UNIT = 1024
    st = ExitStack()

    def sb(name, shape, dt=F32):
        return st.enter_context(nc.sbuf_tensor(f"{name}_m", shape, dt))

    def sem(name):
        return top.enter_context(nc.semaphore(f"{name}_m"))

    with st:
        up = [sb(f"up{h}", [P, KC, FF], F32R) for h in HALVES]
        down = [sb(f"down{h}", [P, FC, H], F32R) for h in HALVES]
        stage = [sb(f"stage{i}", [P, UNIT]) for i in range(2)]
        b1_part = sb("b1_part", [P, FC, 1])
        b2_all = sb("b2_all", [P, H])
        nT = [[sb(f"nT{i}{h}", [P, KC, PR], F32R) for h in HALVES] for i in range(2)]
        g = [sb(f"g{i}", [P, PR]) for i in range(RING)]
        gs = [[sb(f"g{i}{h}", [P, PR], F32R) for h in HALVES] for i in range(RING)]
        resid = [sb(f"resid{t}", [P, H]) for t in range(2)]

        stage_loaded = [sem(f"stage_loaded{i}") for i in range(2)]
        w_hi, w_split, consts_loaded = map(sem, ("w_hi", "w_split", "consts_loaded"))
        J_full = [sem(f"J_full{i}") for i in range(2)]
        J_taken = [sem(f"J_taken{i}") for i in range(2)]
        A_full = [sem(f"A_full{i}") for i in range(4)]
        A_taken = [sem(f"A_taken{i}") for i in range(4)]
        resid_loaded = [sem(f"resid_loaded{t}") for t in range(2)]
        resid_ready = [sem(f"resid_ready{t}") for t in range(2)]
        n_hi, n_split, g_hi, g_split = map(sem, ("n_hi", "n_split", "g_hi", "g_split"))

        PER_PAIR = dict(J=FC, g=FC, pair=1, n=1)

        units = []
        for k in range(KC):
            for u in range(FF // UNIT):
                cols = slice(u * UNIT, (u + 1) * UNIT)
                units.append((1, by_chunk(w1)[:, k:k + 1, cols], [w_[:, k:k + 1, cols] for w_ in up]))
        per = UNIT // H
        for u in range(FC // per):
            ks = slice(u * per, (u + 1) * per)
            units.append((per, by_chunk(w2)[:, ks, :], [w_[:, ks, :] for w_ in down]))

        def staged(u):
            return stage[u % 2][:, :].rearrange("p (k n) -> p k n", k=units[u][0])

        def all_pairs(eng, w, prepare, pair):
            prepare(0, 0)
            with eng.Fori(0, (PAIRS - 2) // 2) as it:
                w.enter(it, 2)
                for t in range(2):
                    pair(it * 2 + t, t, True)
                w.leave((PAIRS - 2) // 2)
            pair(PAIRS - 2, 0, True)
            pair(PAIRS - 1, 1, False)

        with nc.Block() as block:

            @block.sync
            def _(sp):
                for u, (_, frm, _) in enumerate(units):
                    if u >= 2:
                        sp.wait_ge(w_split, u - 1)
                    sp.dma_start(staged(u), frm).then_inc(stage_loaded[u % 2], 16)
                with sp.Fori(0, PAIRS // 2) as it:
                    for t in range(2):
                        for r in range(2):
                            sp.wait_ge(A_taken[2 * (1 - t) + r], it + t + 1)
                            sp.dma_start(resid[r][:, :], x[it * 4 + 2 * t + r]).then_inc(resid_loaded[r], 16)

            @block.gpsimd
            def _(pool):
                pool.dma_start(b2_all[:, :], b2.partition_broadcast(P)).then_inc(consts_loaded, 16)
                with nc.allow_non_contiguous_dma(reason="2048 bias values, one per partition and chunk"):
                    pool.dma_start(b1_part[:, :, :], b1.rearrange("(c p a) -> p c a", p=P, a=1))\
                        .then_inc(consts_loaded, 16)
                pool.wait_ge(consts_loaded, 32)
                with pool.Fori(0, PAIRS) as i:
                    for t in range(2):
                        pool.wait_ge(resid_loaded[t], i * 16 + 16)
                        pool.tensor_tensor(resid[t][:, :], resid[t][:, :], b2_all[:, :], ALU.add)\
                            .then_inc(resid_ready[t], 1)

            @block.scalar
            def _(act):
                w = Walk(PER_PAIR)
                for j in range(2):
                    act.nop().then_inc(J_taken[j], 1)
                for u, (_, _, (hi, _)) in enumerate(units):
                    act.wait_ge(stage_loaded[u % 2], 16 * (u // 2 + 1))
                    nc.scalar.activation(hi, staged(u), ACT.Copy).then_inc(w_hi, 1)
                act.wait_ge(consts_loaded, 32)

                def prepare(i, t):
                    nc.scalar.activation(nT[t][0][:, :, :], between[:, :, bass.ds(i * PR, PR)], ACT.Copy)\
                        .then_inc(n_hi, 1)

                def pair(i, t, ahead):
                    for f in range(FC):
                        j, n = w.use("J", 2)
                        slot = f % RING
                        act.wait_ge(J_full[j], n + 1)
                        nc.scalar.activation(g[slot][:, :], J[j][:, 0:PR], ACT.Gelu_apprx_tanh,
                                             bias=b1_part[:, f, :]).then_inc(J_taken[j], 1)
                        act.wait_ge(J_taken[j], n + 2)
                        nc.scalar.activation(gs[slot][0][:, :], g[slot][:, :], ACT.Copy).then_inc(g_hi, 1)
                        if ahead and f == FC // 2:
                            prepare(i + 1, 1 - t)

                all_pairs(act, w, prepare, pair)

            @block.vector
            def _(dve):
                w = Walk(PER_PAIR)
                for bank in range(SB):
                    dve.nop().then_inc(A_taken[bank], 1)
                for u, (_, _, (hi, lo)) in enumerate(units):
                    dve.wait_ge(w_hi, u + 1)
                    nc.vector.tensor_tensor(lo, staged(u), hi.bitcast(F32), ALU.subtract).then_inc(w_split, 1)

                def prepare(i, t):
                    dve.wait_ge(n_hi, w.event("n"))
                    nc.vector.tensor_tensor(nT[t][1][:, :, :], between[:, :, bass.ds(i * PR, PR)],
                                            nT[t][0][:, :, :].bitcast(F32), ALU.subtract).then_inc(n_split, 1)

                def pair(i, t, ahead):
                    for f in range(FC):
                        slot = f % RING
                        dve.wait_ge(g_hi, w.event("g"))
                        nc.vector.tensor_tensor(gs[slot][1][:, :], g[slot][:, :], gs[slot][0][:, :].bitcast(F32),
                                                ALU.subtract).then_inc(g_split, 1)
                        if ahead and f == FC // 2:
                            prepare(i + 1, 1 - t)
                    _, n = w.use("pair", 2)
                    for r in range(2):
                        bank = 2 * t + r
                        dve.wait_ge(resid_ready[r], i + 1)
                        dve.wait_ge(A_full[bank], n + 1)
                        nc.vector.tensor_tensor(between[:, 2 * r:2 * r + 2, bass.ds(i * PR, PR)],
                                                S[bank][:, :].rearrange("p (a c) -> p a c", a=2),
                                                resid[r][:, :].rearrange("p (a c) -> p a c", a=2), ALU.add)\
                            .then_inc(A_taken[bank], 1)

                all_pairs(dve, w, prepare, pair)

            @block.tensor
            def _(pe):
                w = Walk(PER_PAIR)
                pe.wait_ge(w_split, len(units))

                def prepare(i, t):
                    pass

                def pair(i, t, ahead):
                    _, m = w.use("pair", 2)
                    pe.wait_ge(n_split, i + 1)

                    def up_product(f):
                        j, n = w.use("J", 2)
                        pe.wait_ge(J_taken[j], n + 1)
                        split_product(nc, J[j][:, 0:PR], lambda h, k: up[h][:, k, f * P:(f + 1) * P],
                                      lambda h, k: nT[t][h][:, k, :], KC).then_inc(J_full[j], 1)

                    for f in range(LAG):
                        up_product(f)
                    for f in range(FC):
                        if f + LAG < FC:
                            up_product(f + LAG)
                        pe.wait_ge(g_split, w.event("g"))
                        for r in range(2):
                            bank = 2 * t + r
                            if f == 0:
                                pe.wait_ge(A_taken[bank], m + 1)
                            mm = split_product(nc, S[bank][:, :],
                                               lambda h, k: gs[f % RING][h][:, r * R:(r + 1) * R],
                                               lambda h, k: down[h][:, f, :], 1, f == 0, f == FC - 1)
                            if f == FC - 1:
                                mm.then_inc(A_full[bank], 1)

                all_pairs(pe, w, prepare, pair)


_INS = ["x", "ctx_2048", "mask_BxS2_ik0", "mask_Bx1xSxS2_ff0", "L0_xattn_q_w", "L0_xattn_q_b",
        "L0_xattn_kv_w", "L0_xattn_kv_b", "L0_xattn_out_w", "L0_xattn_out_b", "L0_xattn_postnorm_w",
        "L0_xattn_mlp_w1", "L0_xattn_mlp_b1", "L0_xattn_mlp_w2", "L0_xattn_mlp_b2",
        "L1_xattn_Wq", "L1_xattn_bq", "L1_xattn_Wk", "L1_xattn_bk", "L1_xattn_Wv", "L1_xattn_bv",
        "L1_xattn_Wo", "L1_xattn_bo", "L1_xattn_gamma", "L1_xattn_beta"]
_OUTS = [((B, R, H), "float32")]


def kernel(**inputs):
    import numpy as _np
    import concourse.bacc as _bacc
    from concourse import mybir as _mybir
    from concourse.bass_utils import run_bass_kernel_spmd as _run

    nc = _bacc.Bacc("TRN2", target_bir_lowering=False, num_devices=1)
    arrays, args = {}, []
    for name in _INS:
        a = _np.ascontiguousarray(inputs[name])
        arrays[f"in_{name}"] = a
        args.append(nc.dram_tensor(f"in_{name}", a.shape, _mybir.dt.from_np(a.dtype), kind="ExternalInput").ap())
    for i, (shape, dtype) in enumerate(_OUTS):
        dt = _mybir.dt.from_np(_np.dtype(dtype))
        args.append(nc.dram_tensor(f"out_{i}", shape, dt, kind="ExternalOutput").ap())
    xattn_kernel(nc, *args)
    r = _run(nc, [arrays], core_ids=[0])
    return r.results[0]["out_0"]
```

```python
from contextlib import ExitStack

import concourse.bass as bass
from concourse import mybir

F32 = mybir.dt.float32
F32R = mybir.dt.float32r
I32 = mybir.dt.int32
ALU = mybir.AluOpType
ACT = mybir.ActivationFunctionType
AX = mybir.AxisListType

B, R, H = 16, 128, 512
P = 128
KC = H // P
FF = 4 * H
FC = FF // P
EPS = 1e-6
HEADS0, DH0 = 16, 32
HEADS1, KV1, DH1 = 32, 8, 16
GROUPS1 = HEADS1 // KV1
NEWTON = 3
FAR = 3e38
NEG = -1e30
SB = 4
RC = 2
ROUNDS = KC // RC
HALVES = ("hi", "lo")
PASSES = ((0, 0), (0, 1), (1, 0))


class Walk:

    def __init__(self, per_step):
        self.per_step, self.n, self.it, self.steps = per_step, dict.fromkeys(per_step, 0), None, 0

    def enter(self, it, steps):
        self.it, self.steps, self.entered = it, steps, dict(self.n)

    def leave(self, iterations):
        for name, per in self.per_step.items():
            assert self.n[name] in (self.entered[name], self.entered[name] + per * self.steps), name
            if self.n[name] != self.entered[name]:
                self.n[name] += per * self.steps * (iterations - 1)
        self.it = None

    def so_far(self, name, slots=1, slot=0):
        before = (self.n[name] - slot + slots - 1) // slots
        if self.it is not None:
            assert self.per_step[name] * self.steps % slots == 0
            before = before + self.it * (self.per_step[name] * self.steps // slots)
        return before

    def use(self, name, slots=1):
        slot = self.n[name] % slots
        before = self.so_far(name, slots, slot)
        self.n[name] += 1
        return slot, before

    def event(self, name):
        return self.use(name)[1] + 1


def by_chunk(weight):
    return weight.rearrange("(k p) n -> p k n", p=P)


class Staging:
    SLOTS, SIZE = 3, 1024

    def __init__(self, nc, top, parts):
        self.ring = [top.enter_context(nc.sbuf_tensor(f"staged{i}", [P, self.SIZE], F32))
                     for i in range(self.SLOTS)]
        self.loaded = [top.enter_context(nc.semaphore(f"staged_loaded{i}")) for i in range(self.SLOTS)]
        self.hi = top.enter_context(nc.semaphore("staged_hi"))
        self.split = top.enter_context(nc.semaphore("staged_split"))
        self.units = [unit for part in parts for unit in part]
        self.first = [sum(len(part) for part in parts[:n]) for n in range(len(parts) + 1)]

    def view(self, u):
        return self.ring[u % self.SLOTS][:, :].rearrange("p (k n) -> p k n", n=self.units[u][0])

    def loads(self, u):
        return 16 * sum(len(self.units[v][1]) for v in range(u % self.SLOTS, u + 1, self.SLOTS))

    def splits(self, u):
        return sum(unit[2] for unit in self.units[:u])

    def load(self, sp, u):
        if u >= self.SLOTS:
            sp.wait_ge(self.split, self.splits(u - self.SLOTS + 1))
        for parts, cols, frm in self.units[u][1]:
            to = self.view(u)[parts]
            sp.dma_start(to if cols is None else to[:, :, cols], frm).then_inc(self.loaded[u % self.SLOTS], 16)

    def prefetched(self, n):
        return range(self.first[n], self.first[n] + self.SLOTS)

    def take_hi(self, nc, act, u, targets):
        act.wait_ge(self.loaded[u % self.SLOTS], self.loads(u))
        for view, (hi, _) in targets:
            nc.scalar.activation(hi, view(self.view(u)), ACT.Copy).then_inc(self.hi, 1)

    def take_lo(self, nc, dve, u, targets):
        for n, (view, (hi, lo)) in enumerate(targets):
            dve.wait_ge(self.hi, self.splits(u) + n + 1)
            nc.vector.tensor_tensor(lo, view(self.view(u)), hi.bitcast(F32), ALU.subtract)\
                .then_inc(self.split, 1)


def whole(staged):
    return staged


def split_product(nc, out, stationary, moving, chunks, first=True, last=True):
    for k in range(chunks):
        for a, b in PASSES:
            mm = nc.tensor.matmul(out, stationary(a, k), moving(b, k),
                                  start=first and k == 0 and (a, b) == PASSES[0],
                                  stop=last and k == chunks - 1 and (a, b) == PASSES[-1])
    return mm


def xattn_kernel(nc, x, ctx_rows, key_mask, add_mask, q_w0, q_b0, kv_w0, kv_b0, out_w0, out_b0, post_w0,
                 w1, b1, w2, b2, Wq, bq, Wk, bk, Wv, bv, Wo, bo, gamma, beta, out):
    with ExitStack() as top:
        ident = top.enter_context(nc.sbuf_tensor("ident", [P, P], F32))
        between = top.enter_context(nc.sbuf_tensor("between", [P, KC, B * R], F32))
        S = [top.enter_context(nc.psum_tensor(f"S{j}", [P, 512], F32)) for j in range(SB)]
        J = [top.enter_context(nc.psum_tensor(f"J{j}", [P, 512], F32)) for j in range(2)]
        O = top.enter_context(nc.psum_tensor("O", [P, 512], F32))
        T = top.enter_context(nc.psum_tensor("T", [P, 512], F32))
        banks = (S, J, O, T)

        every = slice(0, P)
        half = [slice(2 * u, 2 * u + 2) for u in range(FC // 2)]
        part0 = [(H, [(every, None, by_chunk(q_w0)[:, half[u]])], 1) for u in range(2)]
        part0 += [(2 * H, [(every, None, by_chunk(kv_w0)[:, k:k + 1])], 2) for k in range(KC)]
        part0 += [(H, [(every, None, by_chunk(out_w0)[:, half[u]])], 1) for u in range(2)]
        part1 = []
        for u in range(FC // 2):
            part1 += [(2 * P, [(every, None, by_chunk(w1)[:, :, u * 2 * P:(u + 1) * 2 * P])], 1),
                      (H, [(every, None, by_chunk(w2)[:, half[u]])], 1)]
        KW1 = KV1 * DH1
        o_rows = Wo.rearrange("(g c d) n -> g d c n", c=GROUPS1, d=DH1)
        part2 = [(H, [(every, None, by_chunk(Wq)[:, half[u]])], 1) for u in range(2)]
        part2 += [(2 * KW1, [(every, slice(0, KW1), by_chunk(Wk)), (every, slice(KW1, 2 * KW1), by_chunk(Wv))], 1)]
        part2 += [(H, [(slice(DH1 * g, DH1 * (g + 1)), None, o_rows[g][:, half[u]]) for g in range(KV1)], 1)
                  for u in range(2)]
        staging = Staging(nc, top, [part0, part1, part2])
        attention(nc, top, staging, 0, ident, between, banks, x, ctx_rows, key_mask, q_b0,
                  (kv_b0,), out_b0, post_w0, None, None)
        mlp(nc, top, staging, between, S, J, x, b1, b2)
        attention(nc, top, staging, 1, ident, between, banks, x, ctx_rows, add_mask, bq,
                  (bk, bv), bo, gamma, beta, out)


def attention(nc, top, staging, L, ident, between, banks, x, ctx_rows, mask, q_b, kv_b, o_b,
              norm_w, norm_b, out):
    S, J, O, T = banks
    st = ExitStack()

    def sb(name, shape, dt=F32):
        return st.enter_context(nc.sbuf_tensor(f"{name}_{L}", shape, dt))

    def sem(name):
        return top.enter_context(nc.semaphore(f"{name}_{L}"))

    keys = 2 * R if L == 0 else R
    per_bank = 512 // keys
    scale = 1.0 / DH0 if L == 0 else float(DH1) ** -0.5
    KW = H if L == 0 else KV1 * DH1
    with st:
        wq = [sb(f"wq{h}", [P, KC, H], F32R) for h in HALVES]
        wo = [sb(f"wo{h}", [P, KC, H], F32R) for h in HALVES]
        if L == 0:
            wk = [sb(f"wk{h}", [P, KC, KW], F32R) for h in HALVES]
            wv = [sb(f"wv{h}", [P, KC, KW], F32R) for h in HALVES]
        else:
            wkv = [sb(f"wkv{h}", [P, KC, 2 * KW], F32R) for h in HALVES]
        bq_all = sb("bq_all", [P, H])
        bo_all = sb("bo_all", [P, H])
        nw_all = sb("nw_all", [P, H])
        bkv_all = sb("bkv_all", [P, 2 * KW])
        if L == 0:
            bk_part = sb("bk_part", [P, KC, 2])
        else:
            nb_all = sb("nb_all", [P, H])
            parity = sb("parity", [P, 2])
        rows = [sb(f"rows{i}", [P, 2, H]) for i in range(2)]
        resid = [sb(f"resid{i}", [P, H]) for i in range(2)]
        hT = [sb(f"hT{h}", [P, KC, 2, R], F32R) for h in HALVES]
        Qn = sb("Qn", [P, H])
        QT = [sb(f"QT{i}", [P, KC, R]) for i in range(2)]
        if L == 0:
            KT = [sb(f"KT{i}", [P, KC, keys]) for i in range(2)]
            V = [sb(f"V{i}", [P, 2, H]) for i in range(2)]
            mrow = [sb(f"mrow{i}", [P, R], I32) for i in range(2)]
            madd = [sb(f"madd{i}", [P, keys]) for i in range(2)]
        else:
            Kn = sb("Kn", [P, KW])
            KT = [sb(f"KT{i}", [P, 2, R]) for i in range(2)]
            V = [sb(f"V{i}", [P, SB, 2, 32]) for i in range(2)]
            madd = [sb(f"madd{i}", [P, R]) for i in range(2)]
        pr = [sb(f"pr{i}", [P, SB, 512]) for i in range(2)]
        nmax = [sb(f"nmax{i}", [P, SB * per_bank]) for i in range(2)]
        den = [sb(f"den{i}", [P, SB * per_bank]) for i in range(2)]
        rec = [sb(f"rec{i}", [P, SB * per_bank]) for i in range(2)]
        pT = sb("pT", [P, SB, 512])
        aT = [[sb(f"aT{i}{h}", [P, KC, R], F32R) for h in HALVES] for i in range(1 + L)]
        res = sb("res", [P, H])
        nrm = sb("nrm", [P, H])
        stat = sb("stat", [P, 16])
        if L == 0:
            squares = sb("squares", [P, H])
        else:
            fin = [sb(f"fin{i}", [P, H]) for i in range(2)]

        consts_loaded, zeroed, prepared = map(sem, ("consts_loaded", "zeroed", "prepared"))
        rows_loaded = [sem(f"rows_loaded{i}") for i in range(2)]
        mask_loaded = [sem(f"mask_loaded{i}") for i in range(2)]
        stored = [sem(f"stored{i}") for i in range(2)]
        J_full = [sem(f"J_full{i}") for i in range(2)]
        J_taken = [sem(f"J_taken{i}") for i in range(2)]
        S_full = [sem(f"S_full{i}") for i in range(SB)]
        S_taken = [sem(f"S_taken{i}") for i in range(SB)]
        O_full, O_taken, T_full, T_taken = map(sem, ("O_full", "O_taken", "T_full", "T_taken"))
        (resid_ready, madd_ready, hT_hi, bank_seen, p_ready, rec_ready, normed, aT_hi, squared,
         small, nrm_ready, scaled, fin_ready) = map(
            sem, ("resid_ready", "madd_ready", "hT_hi", "bank_seen", "p_ready", "rec_ready", "normed",
                  "aT_hi", "squared", "small", "nrm_ready", "scaled", "fin_ready"))

        PER_STEP = dict(J=10 if L == 0 else 6, S=2 * ROUNDS, O=ROUNDS, T=2 - L, entry=1, hT=2,
                        pair=2 * ROUNDS, bank=SB * ROUNDS, aT=ROUNDS, done=1, normed=1,
                        small=(1 if L == 0 else 4) + 2 + 2 * NEWTON)
        ROW_LOADS = 2 if L == 0 else 3
        CONSTS = 16 * (5 if L == 0 else 6)
        PREPARED = 1 if L == 0 else 2

        u0 = staging.first[2 * L]
        targets = {}
        for u in range(2):
            ks = slice(2 * u, 2 * u + 2)
            targets[u0 + u] = [(whole, [w_[:, ks, :] for w_ in wq])]
            targets[staging.first[2 * L + 1] - 2 + u] = [(whole, [w_[:, ks, :] for w_ in wo])]
        if L == 0:
            def take(n):
                return lambda staged: staged.rearrange("p k (f two) -> p k f two", two=2)[:, :, :, n]
            for k in range(KC):
                targets[u0 + 2 + k] = [(take(n), [w_[:, k:k + 1, :] for w_ in ww]) for n, ww in enumerate((wk, wv))]
        else:
            targets[u0 + 2] = [(whole, [w_[:, :, :] for w_ in wkv])]
        end = staging.first[2 * L + 1]
        WEIGHTS = dict(query=range(u0, u0 + 2), key=range(u0 + 2, end - 2), out=range(end - 2, end))

        def prologue(do):
            do["residual"](0, 0)
            for kind in range(2):
                do["turn"](0, 0, kind)
                do["turn_low"](0, 0, kind)
            do["weights"](WEIGHTS["query"])
            do["query"](0, 0)
            do["weights"](WEIGHTS["key"])
            do["key"](0, 0, 0)
            do["turn_query"](0, 0)
            if L == 0:
                for c in range(1, KC):
                    do["key"](0, 0, c)
            else:
                do["turn_key"](0, 0)
            do["projected"](0, 0)
            for pair in range(2):
                do["scores"](0, 0, 0, pair)
                do["mask"](0, 0, 0, pair)
            if L == 0:
                for kind in range(2):
                    do["value"](0, 0, kind)
            do["weights"](WEIGHTS["out"])
            for kind in range(2):
                do["turn"](1, 1, kind)
                do["turn_low"](1, 1, kind)
            do["residual"](1, 1)

        def first_round(do, b, s, ahead, behind):
            o = 1 - s
            do["exp"](b, s, 0, 0)
            do["exp"](b, s, 0, 1)
            if L == 0 and behind:
                do["probs"](b - 1, o, 1)
            if ahead:
                do["query"](b + 1, o)
            do["exp"](b, s, 0, 2)
            if L == 1 and behind:
                do["probs"](b - 1, o, 1)
            do["normalise"](b, s, 0, 0)
            if L == 1 and ahead:
                do["turn_query"](b + 1, o)
            do["exp"](b, s, 0, 3)
            do["scores"](b, s, 1, 0)
            do["mask"](b, s, 1, 0)
            if L == 0 and ahead:
                do["turn_query"](b + 1, o)
                do["key"](b + 1, o, 0)
            if behind:
                do["values"](b - 1, o, 1)
            do["normalise"](b, s, 0, 1)
            if ahead:
                do["key"](b + 1, o, 1 - L)
            do["scores"](b, s, 1, 1)
            do["mask"](b, s, 1, 1)
            if L == 0 and ahead:
                do["key"](b + 1, o, 2)
                do["key"](b + 1, o, 3)

        def second_round(do, b, s, ahead, turned, behind):
            o = 1 - s
            do["exp"](b, s, 1, 0)
            if L == 1:
                if ahead:
                    do["turn_key"](b + 1, o)
                if turned:
                    do["turn"](b + 2, s, 0)
                    do["turn_low"](b + 2, s, 0)
            if behind:
                do["output"](b - 1, o)
            do["exp"](b, s, 1, 1)
            do["exp"](b, s, 1, 2)
            do["probs"](b, s, 0)
            do["normalise"](b, s, 1, 0)
            do["exp"](b, s, 1, 3)
            if behind:
                do["norm"](b - 1, o)
                if ahead:
                    do["residual"](b + 1, o)
            if L == 0 and ahead:
                do["value"](b + 1, o, 0)
            do["normalise"](b, s, 1, 1)
            if ahead:
                do["projected"](b + 1, o)
                do["scores"](b + 1, o, 0, 0)
                do["mask"](b + 1, o, 0, 0)
            if L == 0:
                if ahead:
                    do["value"](b + 1, o, 1)
                if turned:
                    do["turn"](b + 2, s, 0)
            else:
                if turned:
                    do["turn"](b + 2, s, 1)
                    do["turn_low"](b + 2, s, 1)
                do["values"](b, s, 0)
            if ahead:
                do["scores"](b + 1, o, 0, 1)
            if L == 0 and turned:
                do["turn_low"](b + 2, s, 0)
                do["turn"](b + 2, s, 1)
            if ahead:
                do["mask"](b + 1, o, 0, 1)
            if L == 0:
                if turned:
                    do["turn_low"](b + 2, s, 1)
                do["values"](b, s, 0)
                if behind:
                    do["finish"](b - 1, o)

        def entry(do, b, s, ahead=True, turned=True, behind=True):
            first_round(do, b, s, ahead, behind)
            second_round(do, b, s, ahead, turned, behind)

        def all_entries(eng, w, do):
            prologue(do)
            entry(do, 0, 0, behind=False)
            with eng.Fori(0, (B - 4) // 2) as it:
                w.enter(it, 2)
                entry(do, it * 2 + 1, 1)
                entry(do, it * 2 + 2, 0)
                w.leave((B - 4) // 2)
            entry(do, B - 3, 1)
            entry(do, B - 2, 0, turned=False)
            entry(do, B - 1, 1, ahead=False, turned=False)
            do["probs"](B - 1, 1, 1)
            do["values"](B - 1, 1, 1)
            do["output"](B - 1, 1)
            do["norm"](B - 1, 1)
            do["finish"](B - 1, 1)

        with nc.Block() as block:

            @block.sync
            def _(sp):
                def load_rows(b, s):
                    sp.dma_start(rows[s][:, 0, :], ctx_rows[b]).then_inc(rows_loaded[s], 16)
                    if L == 0:
                        sp.dma_start(rows[s][:, 1, :], x[b]).then_inc(rows_loaded[s], 16)
                    else:
                        for a in range(2):
                            sp.dma_start(rows[s][:, 1, a * 256:(a + 1) * 256],
                                         between[:, 2 * s + a, bass.ds((b - s) * R, 256)])\
                                .then_inc(rows_loaded[s], 16)

                def load_mask(b, s):
                    if L == 0:
                        sp.dma_start(mrow[s][:, :], mask[b].partition_broadcast(P)).then_inc(mask_loaded[s], 16)
                    else:
                        sp.dma_start(madd[s][:, :], mask[b, 0]).then_inc(mask_loaded[s], 16)

                def load_next(b, s):
                    entries, halves, used = b + 1, b * 2 + 2, b * (2 * ROUNDS) + 2
                    if not isinstance(b, int):
                        entries, halves, used = sp.snap(entries), sp.snap(halves), sp.snap(used)
                    sp.wait_ge(resid_ready, entries)
                    sp.wait_ge(hT_hi, halves)
                    load_rows(b + 2, s)
                    if L == 0:
                        sp.wait_ge(madd_ready, b + 1)
                    else:
                        sp.wait_ge(S_taken[SB - 1], used)
                    load_mask(b + 2, s)

                def store(b, s):
                    if L == 1:
                        sp.wait_ge(fin_ready, b + 1)
                        sp.dma_start(out[b], fin[s][:, :]).then_inc(stored[s], 16)

                if L == 1:
                    for s in range(2):
                        sp.nop().then_inc(stored[s], 16)
                load_rows(0, 0)
                load_mask(0, 0)
                for u in range(staging.first[2 * L], staging.first[2 * L + 1]):
                    if L == 0 or u not in staging.prefetched(2):
                        staging.load(sp, u)
                load_rows(1, 1)
                load_mask(1, 1)
                load_next(0, 0)
                load_next(1, 1)
                with sp.Fori(0, (B - 4) // 2) as it:
                    for s in range(2):
                        load_next(it * 2 + s + 2, s)
                        store(it * 2 + s, s)
                for b in range(B - 4, B):
                    store(b, b % 2)
                if L == 0:
                    for u in staging.prefetched(1):
                        staging.load(sp, u)
                else:
                    for s in range(2):
                        sp.wait_ge(stored[s], 16 * (B // 2 + 1))

            @block.gpsimd
            def _(pool):
                vectors = [(bq_all[:, :], q_b), (bo_all[:, :], o_b), (nw_all[:, :], norm_w)]
                if L == 0:
                    vectors += [(bkv_all[:, :], kv_b[0])]
                else:
                    vectors += [(bkv_all[:, 0:KW], kv_b[0]), (bkv_all[:, KW:2 * KW], kv_b[1]),
                                (nb_all[:, :], norm_b)]
                for to, frm in vectors:
                    pool.dma_start(to, frm.partition_broadcast(P)).then_inc(consts_loaded, 16)
                if L == 0:
                    pool.dma_start(bk_part[:, :, :], kv_b[0].rearrange("(c p two) -> p c two", p=P, two=2))\
                        .then_inc(consts_loaded, 16)
                    pool.memset(ident[:, :], 0.0).then_inc(zeroed, 1)
                    for s in range(2):
                        pool.memset(madd[s][:, R:2 * R], 0.0).then_inc(zeroed, 1)
                    pool.wait_ge(zeroed, 3)
                    pool.affine_select(out=ident[:, :], in_=ident[:, :], compare_op=ALU.not_equal,
                                       fill=1.0, base=0, pattern=[[-1, P]], channel_multiplier=1)\
                        .then_inc(prepared, 1)
                else:
                    for s in range(2):
                        pool.memset(V[s][:, :, :, :], 0.0).then_inc(prepared, 1)
                pool.wait_ge(consts_loaded, CONSTS)

                w = Walk(PER_STEP)
                if L == 1:
                    pool.nop().then_inc(scaled, 1)

                def normalise(b, s, r, pair):
                    slot = r % 2
                    pool.wait_ge(rec_ready, w.event("pair"))
                    for j in (2 * pair, 2 * pair + 1):
                        part = pr[slot][:, j, :].rearrange("p (h k) -> p h k", k=keys)
                        by = rec[slot][:, j * per_bank:(j + 1) * per_bank]
                        pool.tensor_tensor(part, part, by.unsqueeze(2).broadcast_to([P, per_bank, keys]),
                                           ALU.mult).then_inc(normed, 1)

                def residual(b, s):
                    _, n = w.use("entry", 2)
                    if not isinstance(b, int) or b >= 2:
                        pool.wait_ge(nrm_ready, b - 1)
                    pool.wait_ge(rows_loaded[s], (n + 1) * (16 * ROW_LOADS))
                    pool.tensor_tensor(resid[s][:, :], rows[s][:, 1, :], bo_all[:, :], ALU.add)\
                        .then_inc(resid_ready, 1)

                def norm(b, s):
                    if L == 1:
                        _, n = w.use("done", 2)
                        pool.wait_ge(nrm_ready, b + 1)
                        pool.wait_ge(stored[s], (n + 1) * 16)
                        pool.tensor_tensor(fin[s][:, :], nrm[:, :], nw_all[:, :], ALU.mult).then_inc(scaled, 1)
                        pool.wait_ge(scaled, b + 2)
                        pool.tensor_tensor(fin[s][:, :], fin[s][:, :], nb_all[:, :], ALU.add)\
                            .then_inc(fin_ready, 1)

                def other(*_):
                    pass

                all_entries(pool, w, dict(normalise=normalise, residual=residual, norm=norm, turn=other,
                                          weights=other, query=other, key=other, turn_query=other,
                                          turn_key=other, value=other, scores=other, exp=other, probs=other,
                                          values=other, output=other, finish=other, mask=other,
                                          projected=other, turn_low=other))

            @block.scalar
            def _(act):
                w = Walk(PER_STEP)
                act.wait_ge(consts_loaded, CONSTS)

                def weights(us):
                    for u in us:
                        staging.take_hi(nc, act, u, targets[u])

                def turn(b, s, kind):
                    j, n = w.use("J", 2)
                    act.wait_ge(J_full[j], n + 1)
                    nc.scalar.activation(hT[0][:, :, kind, :], J[j][:, :].rearrange("p (k r) -> p k r", k=KC),
                                         ACT.Copy).then_inc(hT_hi, 1)

                def query(b, s):
                    w.use("J")

                def key(b, s, c):
                    j, n = w.use("J", 2)
                    if L == 0:
                        act.wait_ge(J_full[j], n + 1)
                        nc.scalar.activation(KT[s][:, c, :], J[j][:, 0:keys], ACT.Identity,
                                             bias=bk_part[:, c, 0:1]).then_inc(J_taken[j], 1)

                def value(b, s, kind):
                    w.use("J")

                def turn_query(b, s):
                    _, n = w.use("T")
                    act.wait_ge(T_full, n + 1)
                    nc.scalar.activation(QT[s][:, :, :], T[:, :].rearrange("p (k r) -> p k r", k=KC),
                                         ACT.Copy, scale=scale).then_inc(T_taken, 1)

                def turn_key(b, s):
                    j, n = w.use("J", 2)
                    act.wait_ge(zeroed, 2)
                    act.wait_ge(J_full[j], n + 1)
                    for a in range(2):
                        last = nc.scalar.activation(KT[s][:, a, :], J[j][:, 0:R], ACT.Copy,
                                                    scale=parity[:, a:a + 1])
                    last.then_inc(J_taken[j], 1)

                def scores(b, s, r, pair):
                    if pair == 0:
                        w.use("S")

                scored = {}

                def exp(b, s, r, j):
                    slot = r % 2
                    if j == 0:
                        scored[r] = w.so_far("S")
                    act.wait_ge(S_taken[j], scored[r])
                    for h in range(per_bank):
                        part = pr[slot][:, j, h * keys:(h + 1) * keys]
                        at = slice(j * per_bank + h, j * per_bank + h + 1)
                        last = nc.scalar.activation(part, part, ACT.Exp, bias=nmax[slot][:, at], scale=-1.0,
                                                    accum_out=den[slot][:, at])
                    last.then_inc(p_ready, 1)

                def probs(b, s, r):
                    _, n = w.use("S")
                    for j in range(1, SB, 2):
                        act.wait_ge(S_full[j], n + 1)
                        nc.scalar.activation(pT[:, j, :], S[j][:, :], ACT.Copy).then_inc(S_taken[j], 1)

                def output(b, s):
                    j, n = w.use("J", 2)
                    if L == 0:
                        act.wait_ge(J_taken[j], n + 1)
                        nc.scalar.activation(squares[:, :], res[:, :], ACT.Square, accum_out=stat[:, 0:1])\
                            .then_inc(squared, 1)

                def finish(b, s):
                    if L == 0:
                        _, n = w.use("T")
                        act.wait_ge(T_full, n + 1)
                        nc.scalar.activation(between[:, :, bass.ds(b * R, R)],
                                             T[:, :].rearrange("p (k r) -> p k r", k=KC),
                                             ACT.Copy).then_inc(T_taken, 1)

                def other(*_):
                    pass

                all_entries(act, w, dict(weights=weights, turn=turn, query=query, key=key, value=value,
                                         turn_query=turn_query, turn_key=turn_key, scores=scores, exp=exp,
                                         probs=probs, output=output, finish=finish, normalise=other,
                                         values=other, norm=other, residual=other, mask=other, projected=other,
                                         turn_low=other))

            @block.vector
            def _(dve):
                w = Walk(PER_STEP)
                if L == 1:
                    halves = ident[:, :].rearrange("p (m a d) -> p a m d", a=2, d=DH1)
                    for a in range(2):
                        last = nc.vector.tensor_reduce(parity[:, a:a + 1], halves[:, a], AX.XY, ALU.add)
                        last.then_inc(zeroed, 1)
                dve.wait_ge(consts_loaded, CONSTS)
                dve.wait_ge(prepared, PREPARED)

                def weights(us):
                    for u in us:
                        staging.take_lo(nc, dve, u, targets[u])

                low = {}

                def turn(b, s, kind):
                    low[kind] = w.use("J", 2)

                def turn_low(b, s, kind):
                    if L == 0 and kind == 0:
                        _, n = w.use("entry", 2)
                        dve.wait_ge(mask_loaded[s], (n + 1) * 16)
                        nc.vector.tensor_scalar(madd[s][:, 0:R], mrow[s][:, :], 0.0, NEG, ALU.is_equal,
                                                ALU.mult).then_inc(madd_ready, 1)
                    j, n = low[kind]
                    dve.wait_ge(J_full[j], n + 1)
                    dve.wait_ge(hT_hi, w.event("hT"))
                    nc.vector.tensor_tensor(hT[1][:, :, kind, :], J[j][:, :].rearrange("p (k r) -> p k r", k=KC),
                                            hT[0][:, :, kind, :].bitcast(F32), ALU.subtract)\
                        .then_inc(J_taken[j], 1)

                def query(b, s):
                    j, n = w.use("J", 2)
                    dve.wait_ge(J_full[j], n + 1)
                    if L == 0:
                        nc.vector.tensor_tensor(Qn[:, :], J[j][:, :], bq_all[:, :], ALU.add)\
                            .then_inc(J_taken[j], 1)
                    else:
                        def by_group(t):
                            return t[:, :].rearrange("p (g c d) -> p g c d", c=GROUPS1, d=DH1)
                        nc.vector.tensor_tensor(Qn[:, :].rearrange("p (c g d) -> p g c d", c=GROUPS1, d=DH1),
                                                by_group(J[j]), by_group(bq_all), ALU.add)\
                            .then_inc(J_taken[j], 1)

                def key(b, s, c):
                    j, n = w.use("J", 2)
                    if L == 1:
                        dve.wait_ge(J_full[j], n + 1)
                        nc.vector.tensor_tensor(Kn[:, :], J[j][:, 0:KW], bkv_all[:, 0:KW], ALU.add)
                        for a in range(2):
                            def heads(t):
                                return t[:, KW:2 * KW].rearrange("p (m a d) -> p a m d", a=2, d=DH1)[:, a]
                            last = nc.vector.tensor_tensor(V[s][:, :, a, a * DH1:(a + 1) * DH1],
                                                           heads(J[j]), heads(bkv_all), ALU.add)
                        last.then_inc(J_taken[j], 1)

                def value(b, s, kind):
                    j, n = w.use("J", 2)
                    dve.wait_ge(J_full[j], n + 1)
                    nc.vector.tensor_tensor(V[s][:, kind, :], J[j][:, :],
                                            bkv_all[:, :].rearrange("p (f two) -> p f two", two=2)[:, :, 1],
                                            ALU.add).then_inc(J_taken[j], 1)

                def turn_query(b, s):
                    w.use("T")

                def turn_key(b, s):
                    w.use("J")

                scored = {}

                def scores(b, s, r, pair):
                    if pair == 0:
                        _, scored[r] = w.use("S")

                def mask(b, s, r, pair):
                    slot, n = r % 2, scored[r]
                    if r == 0 and pair == 0:
                        if L == 0:
                            dve.wait_ge(madd_ready, b + 1)
                        else:
                            _, m = w.use("entry", 2)
                            dve.wait_ge(mask_loaded[s], (m + 1) * 16)
                        dve.nop().then_inc(bank_seen, 1)
                    for j in (2 * pair, 2 * pair + 1):
                        dve.wait_ge(S_full[j], n + 1)
                        dve.nop().then_inc(bank_seen, 1)
                        for h in range(per_bank):
                            cols = slice(h * keys, (h + 1) * keys)
                            last = nc.vector.tensor_tensor_reduce(
                                pr[slot][:, j, cols], S[j][:, cols], madd[s][:, :], -1.0, FAR, ALU.add,
                                ALU.min, nmax[slot][:, j * per_bank + h:j * per_bank + h + 1])
                        last.then_inc(S_taken[j], 1)

                def normalise(b, s, r, pair):
                    slot = r % 2
                    sums = slice(pair * 2 * per_bank, (pair + 1) * 2 * per_bank)
                    for j in range(2):
                        last = w.event("bank")
                    dve.wait_ge(p_ready, last)
                    nc.vector.reciprocal(rec[slot][:, sums], den[slot][:, sums]).then_inc(rec_ready, 1)

                def probs(b, s, r):
                    _, n = w.use("S")
                    for j in range(0, SB, 2):
                        dve.wait_ge(S_full[j], n + 1)
                        nc.vector.tensor_copy(pT[:, j, :], S[j][:, :]).then_inc(S_taken[j], 1)

                def values(b, s, r):
                    hi, lo = (t[:, RC * r:RC * (r + 1), :] for t in aT[s if L else 0])
                    result = O[:, 0:RC * R].rearrange("p (c r) -> p c r", c=RC)
                    _, n = w.use("O")
                    dve.wait_ge(O_full, n + 1)
                    nc.vector.tensor_copy(hi, result).then_inc(aT_hi, 1)
                    dve.wait_ge(aT_hi, w.event("aT"))
                    nc.vector.tensor_tensor(lo, result, hi.bitcast(F32), ALU.subtract).then_inc(O_taken, 1)

                added = []

                def output(b, s):
                    j, n = w.use("J", 2)
                    added[:] = [(J_taken[j], n + 1)]
                    dve.wait_ge(resid_ready, b + 1)
                    dve.wait_ge(J_full[j], n + 1)
                    nc.vector.tensor_tensor(res[:, :], J[j][:, :], resid[s][:, :], ALU.add)\
                        .then_inc(J_taken[j], 1)

                def inverse_root():
                    m, y, t, h = (stat[:, c:c + 1] for c in (1, 2, 3, 10))
                    nc.vector.tensor_scalar(h, m, -0.5, None, ALU.mult)
                    nc.vector.tensor_scalar(t.bitcast(I32), m.bitcast(I32), 1, None, ALU.logical_shift_right)\
                        .then_inc(small, 1)
                    dve.wait_ge(small, w.event("small"))
                    nc.vector.tensor_scalar(y.bitcast(I32), t.bitcast(I32), -1.0, float(0x5F3759DF), ALU.mult,
                                            ALU.add).then_inc(small, 1)
                    dve.wait_ge(small, w.event("small"))
                    for _ in range(NEWTON):
                        nc.vector.scalar_tensor_tensor(t, y, h, y, ALU.mult, ALU.mult).then_inc(small, 1)
                        dve.wait_ge(small, w.event("small"))
                        nc.vector.scalar_tensor_tensor(y, t, 1.5, y, ALU.add, ALU.mult).then_inc(small, 1)
                        dve.wait_ge(small, w.event("small"))

                def norm(b, s):
                    done = w.event("normed")
                    if L == 0:
                        dve.wait_ge(squared, done)
                        nc.vector.tensor_scalar(stat[:, 1:2], stat[:, 0:1], 1.0 / H, EPS, ALU.mult, ALU.add)\
                            .then_inc(small, 1)
                        dve.wait_ge(small, w.event("small"))
                        inverse_root()
                        nc.vector.scalar_tensor_tensor(nrm[:, :], res[:, :], stat[:, 2:3], nw_all[:, :],
                                                       ALU.mult, ALU.mult).then_inc(nrm_ready, 1)
                    else:
                        dve.wait_ge(*added[0])
                        nc.vector.bn_stats(stat[:, 4:10], res[:, :]).then_inc(small, 1)
                        dve.wait_ge(small, w.event("small"))
                        mean_e, var_e, mean_o, var_o, gap, var = (
                            stat[:, c:c + 1] for c in (5, 6, 8, 9, 11, 12))
                        nc.vector.tensor_tensor(stat[:, 0:1], mean_e, mean_o, ALU.add)
                        nc.vector.scalar_tensor_tensor(var, var_e, H * EPS, var_o, ALU.add, ALU.add)
                        nc.vector.tensor_tensor(gap, mean_e, mean_o, ALU.subtract).then_inc(small, 1)
                        dve.wait_ge(small, w.event("small"))
                        nc.vector.tensor_scalar(stat[:, 0:1], stat[:, 0:1], 0.5, None, ALU.mult)
                        nc.vector.scalar_tensor_tensor(stat[:, 13:14], gap, 0.25, gap, ALU.mult, ALU.mult)\
                            .then_inc(small, 1)
                        dve.wait_ge(small, w.event("small"))
                        nc.vector.scalar_tensor_tensor(stat[:, 1:2], var, 1.0 / H, stat[:, 13:14], ALU.mult,
                                                       ALU.add).then_inc(small, 1)
                        dve.wait_ge(small, w.event("small"))
                        inverse_root()
                        dve.wait_ge(scaled, done)
                        nc.vector.tensor_scalar(nrm[:, :], res[:, :], stat[:, 0:1], stat[:, 2:3],
                                                ALU.subtract, ALU.mult).then_inc(nrm_ready, 1)

                def finish(b, s):
                    if L == 0:
                        w.use("T")

                def other(*_):
                    pass

                all_entries(dve, w, dict(weights=weights, turn=turn, query=query, key=key, value=value,
                                         turn_query=turn_query, turn_key=turn_key, scores=scores,
                                         normalise=normalise, probs=probs, values=values, output=output,
                                         norm=norm, finish=finish, exp=other, residual=other, mask=mask,
                                         projected=other, turn_low=turn_low))

            @block.tensor
            def _(pe):
                w = Walk(PER_STEP)
                pe.wait_ge(prepared, PREPARED)

                def weights(us):
                    pe.wait_ge(staging.split, staging.splits(us[-1] + 1))

                def turn(b, s, kind):
                    if kind == 0:
                        _, e = w.use("entry", 2)
                        pe.wait_ge(rows_loaded[s], (e + 1) * (16 * ROW_LOADS))
                    j, n = w.use("J", 2)
                    pe.wait_ge(J_taken[j], n)
                    for k in range(KC):
                        mm = nc.tensor.transpose(J[j][:, k * R:(k + 1) * R], rows[s][:, kind, k * P:(k + 1) * P],
                                                 ident[:, :])
                    mm.then_inc(J_full[j], 1)

                natural = {}

                def query(b, s):
                    for i in range(2):
                        pe.wait_ge(J_taken[i], w.so_far("J", 2, i))
                    j, n = w.use("J", 2)
                    natural["query"] = (J_taken[j], n + 1)
                    pe.wait_ge(J_taken[j], n)
                    split_product(nc, J[j][:, :], lambda h, k: hT[h][:, k, 1, :], lambda h, k: wq[h][:, k, :], KC)\
                        .then_inc(J_full[j], 1)

                def key(b, s, c):
                    j, n = w.use("J", 2)
                    natural["key"] = natural[c % 2] = (J_taken[j], n + 1)
                    pe.wait_ge(J_taken[j], n)
                    if L == 0:
                        mm = split_product(nc, J[j][:, 0:keys], lambda h, k: wk[h][:, k, c * P:(c + 1) * P],
                                           lambda h, k: hT[h][:, k, :, :], KC)
                    else:
                        mm = split_product(nc, J[j][:, 0:2 * KW], lambda h, k: hT[h][:, k, 0, :],
                                           lambda h, k: wkv[h][:, k, :], KC)
                    mm.then_inc(J_full[j], 1)

                def value(b, s, kind):
                    j, n = w.use("J", 2)
                    pe.wait_ge(J_taken[j], n)
                    split_product(nc, J[j][:, :], lambda h, k: hT[h][:, k, kind, :],
                                  lambda h, k: wv[h][:, k, :], KC).then_inc(J_full[j], 1)

                def turn_query(b, s):
                    pe.wait_ge(*natural["query"])
                    _, n = w.use("T")
                    natural["turned"] = (T_taken, n + 1)
                    pe.wait_ge(T_taken, n)
                    for c in range(KC):
                        mm = nc.tensor.transpose(T[:, c * R:(c + 1) * R], Qn[:, c * P:(c + 1) * P], ident[:, :])
                    mm.then_inc(T_full, 1)

                def turn_key(b, s):
                    pe.wait_ge(*natural["key"])
                    j, n = w.use("J", 2)
                    natural[0] = natural[1] = (J_taken[j], n + 1)
                    pe.wait_ge(J_taken[j], n)
                    nc.tensor.transpose(J[j][:, 0:R], Kn[:, :], ident[:, :]).then_inc(J_full[j], 1)

                def projected(b, s):
                    for name in ("turned", 0, 1):
                        pe.wait_ge(*natural[name])

                scored = {}

                def scores(b, s, r, pair):
                    if pair == 0:
                        _, scored[r] = w.use("S")
                    n = scored[r]
                    for c in range(RC):
                        for j in (2 * pair, 2 * pair + 1):
                            if c == 0:
                                pe.wait_ge(S_taken[j], n)
                            strip = slice(32 * j, 32 * (j + 1))
                            k_ap = KT[s][strip, RC * r + c, :] if L == 0 else KT[s][strip, :, :]
                            mm = nc.tensor.matmul(S[j][:, c * 256:(c + 1) * 256], QT[s][strip, RC * r + c, :],
                                                  k_ap, start=True, stop=True)
                            if c == RC - 1:
                                mm.then_inc(S_full[j], 1)

                turned = {}

                def probs(b, s, r):
                    slot = r % 2
                    _, n = w.use("S")
                    turned[r] = n
                    for j in range(SB):
                        pe.wait_ge(normed, w.event("bank"))
                        pe.wait_ge(S_taken[j], n)
                        for q in range(4):
                            to = q if L == 0 else (q % 2) * 2 + q // 2
                            mm = nc.tensor.transpose(S[j][:, to * P:(to + 1) * P],
                                                     pr[slot][:, j, q * P:(q + 1) * P], ident[:, :])
                        mm.then_inc(S_full[j], 1)

                def values(b, s, r):
                    _, n = w.use("O")
                    pe.wait_ge(O_taken, n)
                    for j in range(SB):
                        pe.wait_ge(S_taken[j], turned[r] + 1)
                    if L == 0:
                        for c in range(RC):
                            for kind in range(2):
                                for j in range(SB):
                                    head = 4 * (RC * r + c) + j
                                    at = (c * 2 + kind) * R
                                    mm = nc.tensor.matmul(O[32 * j:32 * (j + 1), c * R:(c + 1) * R],
                                                          V[s][:, kind, head * DH0:(head + 1) * DH0],
                                                          pT[:, j, at:at + R], start=kind == 0, stop=kind == 1)
                    else:
                        for a in range(2):
                            for j in range(SB):
                                mm = nc.tensor.matmul(O[32 * j:32 * (j + 1), 0:RC * R], V[s][:, j, a, :],
                                                      pT[:, j, a * RC * R:(a + 1) * RC * R],
                                                      start=a == 0, stop=a == 1)
                    mm.then_inc(O_full, 1)

                def output(b, s):
                    pe.wait_ge(O_taken, w.event("done") * ROUNDS)
                    j, n = w.use("J", 2)
                    pe.wait_ge(J_taken[j], n)
                    split_product(nc, J[j][:, :], lambda h, k: aT[s if L else 0][h][:, k, :], lambda h, k: wo[h][:, k, :], KC)\
                        .then_inc(J_full[j], 1)

                def finish(b, s):
                    if L == 0:
                        _, n = w.use("T")
                        pe.wait_ge(T_taken, n)
                        pe.wait_ge(nrm_ready, w.so_far("done"))
                        for k in range(KC):
                            mm = nc.tensor.transpose(T[:, k * R:(k + 1) * R], nrm[:, k * P:(k + 1) * P], ident[:, :])
                        mm.then_inc(T_full, 1)

                def other(*_):
                    pass

                all_entries(pe, w, dict(weights=weights, turn=turn, query=query, key=key, value=value,
                                        turn_query=turn_query, turn_key=turn_key, scores=scores,
                                        probs=probs, values=values, output=output, finish=finish,
                                        normalise=other, exp=other, norm=other, residual=other,
                                        mask=other, projected=projected, turn_low=other))


def mlp(nc, top, staging, between, S, J, x, b1, b2):
    PAIRS, PR = B // 2, 2 * R
    LAG = 2
    RING = 4
    st = ExitStack()

    def sb(name, shape, dt=F32):
        return st.enter_context(nc.sbuf_tensor(f"{name}_m", shape, dt))

    def sem(name):
        return top.enter_context(nc.semaphore(f"{name}_m"))

    with st:
        up = [sb(f"up{h}", [P, KC, FF], F32R) for h in HALVES]
        down = [sb(f"down{h}", [P, FC, H], F32R) for h in HALVES]
        b1_part = sb("b1_part", [P, FC, 1])
        b2_all = sb("b2_all", [P, H])
        nT = [[sb(f"nT{i}{h}", [P, KC, PR], F32R) for h in HALVES] for i in range(2)]
        g = [sb(f"g{i}", [P, PR]) for i in range(RING)]
        gs = [[sb(f"g{i}{h}", [P, PR], F32R) for h in HALVES] for i in range(RING)]
        resid = [sb(f"resid{t}", [P, H]) for t in range(2)]

        consts_loaded = sem("consts_loaded")
        J_full = [sem(f"J_full{i}") for i in range(2)]
        J_taken = [sem(f"J_taken{i}") for i in range(2)]
        A_full = [sem(f"A_full{i}") for i in range(4)]
        A_taken = [sem(f"A_taken{i}") for i in range(4)]
        resid_loaded = [sem(f"resid_loaded{t}") for t in range(2)]
        resid_ready = [sem(f"resid_ready{t}") for t in range(2)]
        n_hi, n_split, g_hi, g_split = map(sem, ("n_hi", "n_split", "g_hi", "g_split"))

        PER_PAIR = dict(J=FC, g=FC, pair=1, n=1)

        u0 = staging.first[1]
        targets = {}
        for v in range(FC // 2):
            targets[u0 + 2 * v] = [(whole, [w_[:, :, v * 2 * P:(v + 1) * 2 * P] for w_ in up])]
            targets[u0 + 2 * v + 1] = [(whole, [w_[:, 2 * v:2 * v + 2, :] for w_ in down])]
        EARLY = 4

        def all_pairs(eng, w, prepare, pair):
            prepare(0, 0)
            pair(0, 0, True, True)
            with eng.Fori(0, (PAIRS - 2) // 2) as it:
                w.enter(it, 2)
                pair(it * 2 + 1, 1, True, False)
                pair(it * 2 + 2, 0, True, False)
                w.leave((PAIRS - 2) // 2)
            pair(PAIRS - 1, 1, False, False)

        with nc.Block() as block:

            @block.sync
            def _(sp):
                for r in range(2):
                    sp.dma_start(resid[r][:, :], x[r]).then_inc(resid_loaded[r], 16)
                for u in range(staging.first[1], staging.first[2]):
                    if u not in staging.prefetched(1):
                        staging.load(sp, u)
                def load_residual(i, t, taken):
                    for r in range(2):
                        sp.wait_ge(A_taken[2 * (1 - t) + r], taken)
                        sp.dma_start(resid[r][:, :], x[i * 2 + r]).then_inc(resid_loaded[r], 16)

                with sp.Fori(0, (PAIRS - 2) // 2) as it:
                    load_residual(it * 2 + 1, 1, it + 2)
                    load_residual(it * 2 + 2, 0, it + 2)
                load_residual(PAIRS - 1, 1, PAIRS // 2 + 1)
                for u in staging.prefetched(2):
                    staging.load(sp, u)

            @block.gpsimd
            def _(pool):
                pool.dma_start(b2_all[:, :], b2.partition_broadcast(P)).then_inc(consts_loaded, 16)
                with nc.allow_non_contiguous_dma(reason="2048 bias values, one per partition and chunk"):
                    pool.dma_start(b1_part[:, :, :], b1.rearrange("(c p a) -> p c a", p=P, a=1))\
                        .then_inc(consts_loaded, 16)
                pool.wait_ge(consts_loaded, 32)
                with pool.Fori(0, PAIRS) as i:
                    for t in range(2):
                        pool.wait_ge(resid_loaded[t], i * 16 + 16)
                        pool.tensor_tensor(resid[t][:, :], resid[t][:, :], b2_all[:, :], ALU.add)\
                            .then_inc(resid_ready[t], 1)

            @block.scalar
            def _(act):
                w = Walk(PER_PAIR)
                act.wait_ge(consts_loaded, 32)

                def prepare(i, t):
                    nc.scalar.activation(nT[t][0][:, :, :], between[:, :, bass.ds(i * PR, PR)], ACT.Copy)\
                        .then_inc(n_hi, 1)

                def pair(i, t, ahead, first):
                    if first:
                        for u in range(EARLY):
                            staging.take_hi(nc, act, u0 + u, targets[u0 + u])
                    for f in range(FC):
                        if first and f + EARLY < 2 * (FC // 2):
                            staging.take_hi(nc, act, u0 + f + EARLY, targets[u0 + f + EARLY])
                        j, n = w.use("J", 2)
                        slot = f % RING
                        act.wait_ge(J_full[j], n + 1)
                        nc.scalar.activation(g[slot][:, :], J[j][:, 0:PR], ACT.Gelu_apprx_tanh,
                                             bias=b1_part[:, f, :]).then_inc(J_taken[j], 1)
                        act.wait_ge(J_taken[j], n + 1)
                        nc.scalar.activation(gs[slot][0][:, :], g[slot][:, :], ACT.Copy).then_inc(g_hi, 1)
                        if ahead and f == FC // 2:
                            prepare(i + 1, 1 - t)

                all_pairs(act, w, prepare, pair)

            @block.vector
            def _(dve):
                w = Walk(PER_PAIR)
                for bank in range(SB):
                    dve.nop().then_inc(A_taken[bank], 1)

                def prepare(i, t):
                    dve.wait_ge(n_hi, w.event("n"))
                    nc.vector.tensor_tensor(nT[t][1][:, :, :], between[:, :, bass.ds(i * PR, PR)],
                                            nT[t][0][:, :, :].bitcast(F32), ALU.subtract).then_inc(n_split, 1)

                def pair(i, t, ahead, first):
                    if first:
                        for u in range(EARLY):
                            staging.take_lo(nc, dve, u0 + u, targets[u0 + u])
                    for f in range(FC):
                        if first and f + EARLY < 2 * (FC // 2):
                            staging.take_lo(nc, dve, u0 + f + EARLY, targets[u0 + f + EARLY])
                        slot = f % RING
                        dve.wait_ge(g_hi, w.event("g"))
                        nc.vector.tensor_tensor(gs[slot][1][:, :], g[slot][:, :], gs[slot][0][:, :].bitcast(F32),
                                                ALU.subtract).then_inc(g_split, 1)
                        if ahead and f == FC // 2:
                            prepare(i + 1, 1 - t)
                    _, n = w.use("pair", 2)
                    for r in range(2):
                        bank = 2 * t + r
                        dve.wait_ge(resid_ready[r], i + 1)
                        dve.wait_ge(A_full[bank], n + 1)
                        nc.vector.tensor_tensor(between[:, 2 * r:2 * r + 2, bass.ds(i * PR, PR)],
                                                S[bank][:, :].rearrange("p (a c) -> p a c", a=2),
                                                resid[r][:, :].rearrange("p (a c) -> p a c", a=2), ALU.add)\
                            .then_inc(A_taken[bank], 1)

                all_pairs(dve, w, prepare, pair)

            @block.tensor
            def _(pe):
                w = Walk(PER_PAIR)

                def prepare(i, t):
                    pass

                def pair(i, t, ahead, first):
                    _, m = w.use("pair", 2)
                    pe.wait_ge(n_split, i + 1)

                    def up_product(f):
                        j, n = w.use("J", 2)
                        pe.wait_ge(J_taken[j], n)
                        if first:
                            pe.wait_ge(staging.split, staging.splits(u0 + 2 * (f // 2) + 1))
                        split_product(nc, J[j][:, 0:PR], lambda h, k: up[h][:, k, f * P:(f + 1) * P],
                                      lambda h, k: nT[t][h][:, k, :], KC).then_inc(J_full[j], 1)

                    for f in range(LAG):
                        up_product(f)
                    for f in range(FC):
                        if f + LAG < FC:
                            up_product(f + LAG)
                        pe.wait_ge(g_split, w.event("g"))
                        if first:
                            pe.wait_ge(staging.split, staging.splits(u0 + 2 * (f // 2) + 2))
                        for r in range(2):
                            bank = 2 * t + r
                            if f == 0:
                                pe.wait_ge(A_taken[bank], m + 1)
                            mm = split_product(nc, S[bank][:, :],
                                               lambda h, k: gs[f % RING][h][:, r * R:(r + 1) * R],
                                               lambda h, k: down[h][:, f, :], 1, f == 0, f == FC - 1)
                            if f == FC - 1:
                                mm.then_inc(A_full[bank], 1)

                all_pairs(pe, w, prepare, pair)


_INS = ["x", "ctx_2048", "mask_BxS2_ik0", "mask_Bx1xSxS2_ff0", "L0_xattn_q_w", "L0_xattn_q_b",
        "L0_xattn_kv_w", "L0_xattn_kv_b", "L0_xattn_out_w", "L0_xattn_out_b", "L0_xattn_postnorm_w",
        "L0_xattn_mlp_w1", "L0_xattn_mlp_b1", "L0_xattn_mlp_w2", "L0_xattn_mlp_b2",
        "L1_xattn_Wq", "L1_xattn_bq", "L1_xattn_Wk", "L1_xattn_bk", "L1_xattn_Wv", "L1_xattn_bv",
        "L1_xattn_Wo", "L1_xattn_bo", "L1_xattn_gamma", "L1_xattn_beta"]
_OUTS = [((B, R, H), "float32")]


def kernel(**inputs):
    import numpy as _np
    import concourse.bacc as _bacc
    from concourse import mybir as _mybir
    from concourse.bass_utils import run_bass_kernel_spmd as _run

    nc = _bacc.Bacc("TRN2", target_bir_lowering=False, num_devices=1)
    arrays, args = {}, []
    for name in _INS:
        a = _np.ascontiguousarray(inputs[name])
        arrays[f"in_{name}"] = a
        args.append(nc.dram_tensor(f"in_{name}", a.shape, _mybir.dt.from_np(a.dtype), kind="ExternalInput").ap())
    for i, (shape, dtype) in enumerate(_OUTS):
        dt = _mybir.dt.from_np(_np.dtype(dtype))
        args.append(nc.dram_tensor(f"out_{i}", shape, dt, kind="ExternalOutput").ap())
    xattn_kernel(nc, *args)
    r = _run(nc, [arrays], core_ids=[0])
    return r.results[0]["out_0"]
```

```python
from contextlib import ExitStack

import concourse.bass as bass
from concourse import mybir

F32 = mybir.dt.float32
F32R = mybir.dt.float32r
I32 = mybir.dt.int32
ALU = mybir.AluOpType
ACT = mybir.ActivationFunctionType
AX = mybir.AxisListType

B, R, H = 16, 128, 512
P = 128
KC = H // P
FF = 4 * H
FC = FF // P
EPS = 1e-6
HEADS0, DH0 = 16, 32
HEADS1, KV1, DH1 = 32, 8, 16
GROUPS1 = HEADS1 // KV1
NEWTON = 3
FAR = 3.4028234e38
NEG = -1e30
SB = 4
RC = 2
ROUNDS = KC // RC
HALVES = ("hi", "lo")
PASSES = ((0, 0), (0, 1), (1, 0))


class Walk:

    def __init__(self, per_step):
        self.per_step, self.n, self.it, self.steps = per_step, dict.fromkeys(per_step, 0), None, 0

    def enter(self, it, steps):
        self.it, self.steps, self.entered = it, steps, dict(self.n)

    def leave(self, iterations):
        for name, per in self.per_step.items():
            assert self.n[name] in (self.entered[name], self.entered[name] + per * self.steps), name
            if self.n[name] != self.entered[name]:
                self.n[name] += per * self.steps * (iterations - 1)
        self.it = None

    def so_far(self, name, slots=1, slot=0):
        before = (self.n[name] - slot + slots - 1) // slots
        if self.it is not None:
            assert self.per_step[name] * self.steps % slots == 0
            before = before + self.it * (self.per_step[name] * self.steps // slots)
        return before

    def use(self, name, slots=1):
        slot = self.n[name] % slots
        before = self.so_far(name, slots, slot)
        self.n[name] += 1
        return slot, before

    def event(self, name):
        return self.use(name)[1] + 1


def by_chunk(weight):
    return weight.rearrange("(k p) n -> p k n", p=P)


class Staging:
    SLOTS, SIZE = 3, 1024

    def __init__(self, nc, top, parts, wide):
        self.units = [unit for part in parts for unit in part]
        self.first = [sum(len(part) for part in parts[:n]) for n in range(len(parts) + 1)]
        ring = [top.enter_context(nc.sbuf_tensor(f"staged{i}", [P, self.SIZE], F32))[:, :]
                for i in range(self.SLOTS)]
        self.buffers = ring + [wide[:, u * self.SIZE:(u + 1) * self.SIZE] for u in range(self.first[1])]
        self.loaded = [top.enter_context(nc.semaphore(f"staged_loaded{i}")) for i in range(len(self.buffers))]
        self.hi = top.enter_context(nc.semaphore("staged_hi"))
        self.split = top.enter_context(nc.semaphore("staged_split"))

    def slot(self, u):
        return self.SLOTS + u if u < self.first[1] else (u - self.first[1]) % self.SLOTS

    def sharing(self, u):
        return [v for v in range(u + 1) if self.slot(v) == self.slot(u)]

    def view(self, u):
        return self.buffers[self.slot(u)].rearrange("p (k n) -> p k n", n=self.units[u][0])

    def loads(self, u):
        return 16 * sum(len(self.units[v][1]) for v in self.sharing(u))

    def splits(self, u):
        return sum(unit[2] for unit in self.units[:u])

    def load(self, sp, u):
        before = self.sharing(u)[:-1]
        if before:
            sp.wait_ge(self.split, self.splits(before[-1] + 1))
        for parts, cols, frm in self.units[u][1]:
            to = self.view(u)[parts]
            sp.dma_start(to if cols is None else to[:, :, cols], frm).then_inc(self.loaded[self.slot(u)], 16)

    def prefetched(self, n):
        return range(self.first[n], self.first[n] + self.SLOTS)

    def take_hi(self, nc, act, u, targets):
        act.wait_ge(self.loaded[self.slot(u)], self.loads(u))
        for view, (hi, _) in targets:
            nc.scalar.activation(hi, view(self.view(u)), ACT.Copy).then_inc(self.hi, 1)

    def take_lo(self, nc, dve, u, targets):
        for n, (view, (hi, lo)) in enumerate(targets):
            dve.wait_ge(self.hi, self.splits(u) + n + 1)
            nc.vector.tensor_tensor(lo, view(self.view(u)), hi.bitcast(F32), ALU.subtract)\
                .then_inc(self.split, 1)


def whole(staged):
    return staged


def split_product(nc, out, stationary, moving, chunks, first=True, last=True):
    for k in range(chunks):
        for a, b in PASSES:
            mm = nc.tensor.matmul(out, stationary(a, k), moving(b, k),
                                  start=first and k == 0 and (a, b) == PASSES[0],
                                  stop=last and k == chunks - 1 and (a, b) == PASSES[-1])
    return mm


def xattn_kernel(nc, x, ctx_rows, key_mask, add_mask, q_w0, q_b0, kv_w0, kv_b0, out_w0, out_b0, post_w0,
                 w1, b1, w2, b2, Wq, bq, Wk, bk, Wv, bv, Wo, bo, gamma, beta, out):
    with ExitStack() as top:
        ident = top.enter_context(nc.sbuf_tensor("ident", [P, P], F32))
        between = top.enter_context(nc.sbuf_tensor("between", [P, KC, B * R], F32))
        S = [top.enter_context(nc.psum_tensor(f"S{j}", [P, 512], F32)) for j in range(SB)]
        J = [top.enter_context(nc.psum_tensor(f"J{j}", [P, 512], F32)) for j in range(2)]
        O = top.enter_context(nc.psum_tensor("O", [P, 512], F32))
        T = top.enter_context(nc.psum_tensor("T", [P, 512], F32))
        banks = (S, J, O, T)

        every = slice(0, P)
        half = [slice(2 * u, 2 * u + 2) for u in range(FC // 2)]
        part0 = [(H, [(every, None, by_chunk(q_w0)[:, half[u]])], 1) for u in range(2)]
        part0 += [(2 * H, [(every, None, by_chunk(kv_w0)[:, k:k + 1])], 2) for k in range(KC)]
        part0 += [(H, [(every, None, by_chunk(out_w0)[:, half[u]])], 1) for u in range(2)]
        part1 = []
        for u in range(FC // 2):
            part1 += [(2 * P, [(every, None, by_chunk(w1)[:, :, u * 2 * P:(u + 1) * 2 * P])], 1),
                      (H, [(every, None, by_chunk(w2)[:, half[u]])], 1)]
        KW1 = KV1 * DH1
        o_rows = Wo.rearrange("(g c d) n -> g d c n", c=GROUPS1, d=DH1)
        part2 = [(H, [(every, None, by_chunk(Wq)[:, half[u]])], 1) for u in range(2)]
        part2 += [(2 * KW1, [(every, slice(0, KW1), by_chunk(Wk)), (every, slice(KW1, 2 * KW1), by_chunk(Wv))], 1)]
        part2 += [(H, [(slice(DH1 * g, DH1 * (g + 1)), None, o_rows[g][:, half[u]]) for g in range(KV1)], 1)
                  for u in range(2)]
        staging = Staging(nc, top, [part0, part1, part2], between[:, :, :].rearrange("p k r -> p (k r)"))
        attention(nc, top, staging, 0, ident, between, banks, x, ctx_rows, key_mask, q_b0,
                  (kv_b0,), out_b0, post_w0, None, None)
        mlp(nc, top, staging, between, S, J, x, b1, b2)
        attention(nc, top, staging, 1, ident, between, banks, x, ctx_rows, add_mask, bq,
                  (bk, bv), bo, gamma, beta, out)


def attention(nc, top, staging, L, ident, between, banks, x, ctx_rows, mask, q_b, kv_b, o_b,
              norm_w, norm_b, out):
    S, J, O, T = banks
    st = ExitStack()

    def sb(name, shape, dt=F32):
        return st.enter_context(nc.sbuf_tensor(f"{name}_{L}", shape, dt))

    def sem(name):
        return top.enter_context(nc.semaphore(f"{name}_{L}"))

    keys = 2 * R if L == 0 else R
    per_bank = 512 // keys
    scale = 1.0 / DH0 if L == 0 else float(DH1) ** -0.5
    KW = H if L == 0 else KV1 * DH1
    with st:
        wq = [sb(f"wq{h}", [P, KC, H], F32R) for h in HALVES]
        wo = [sb(f"wo{h}", [P, KC, H], F32R) for h in HALVES]
        if L == 0:
            wk = [sb(f"wk{h}", [P, KC, KW], F32R) for h in HALVES]
            wv = [sb(f"wv{h}", [P, KC, KW], F32R) for h in HALVES]
        else:
            wkv = [sb(f"wkv{h}", [P, KC, 2 * KW], F32R) for h in HALVES]
        bq_all = sb("bq_all", [P, H])
        bo_all = sb("bo_all", [P, H])
        nw_all = sb("nw_all", [P, H])
        bkv_all = sb("bkv_all", [P, 2 * KW])
        if L == 0:
            bk_part = sb("bk_part", [P, KC, 2])
        else:
            nb_all = sb("nb_all", [P, H])
            parity = sb("parity", [P, 2])
        rows = [sb(f"rows{i}", [P, 2, H]) for i in range(2)]
        resid = [sb(f"resid{i}", [P, H]) for i in range(2)]
        hT = [sb(f"hT{h}", [P, KC, 2, R], F32R) for h in HALVES]
        Qn = sb("Qn", [P, H])
        QT = [[sb(f"QT{i}{h}", [P, KC, R], F32R) for h in HALVES] for i in range(2)]
        if L == 0:
            KT = [[sb(f"KT{i}{h}", [P, KC, keys], F32R) for h in HALVES] for i in range(2)]
            V = [sb(f"V{i}", [P, 2, H]) for i in range(2)]
            mrow = [sb(f"mrow{i}", [P, R], I32) for i in range(2)]
            madd = [sb(f"madd{i}", [P, keys]) for i in range(2)]
        else:
            Kn = sb("Kn", [P, KW])
            KT = [[sb(f"KT{i}{h}", [P, 2, R], F32R) for h in HALVES] for i in range(2)]
            V = [sb(f"V{i}", [P, SB, 2, 32]) for i in range(2)]
            madd = [sb(f"madd{i}", [P, R]) for i in range(2)]
        pr = [sb(f"pr{i}", [P, SB, 512]) for i in range(2)]
        nmax = [sb(f"nmax{i}", [P, SB * per_bank]) for i in range(2)]
        den = [sb(f"den{i}", [P, SB * per_bank]) for i in range(2)]
        rec = [sb(f"rec{i}", [P, SB * per_bank]) for i in range(2)]
        pT = sb("pT", [P, SB, 512])
        aT = [[sb(f"aT{i}{h}", [P, KC, R], F32R) for h in HALVES] for i in range(1 + L)]
        res = sb("res", [P, H])
        nrm = sb("nrm", [P, H])
        stat = sb("stat", [P, 16])
        if L == 1:
            three_halves = sb("three_halves", [P, 1])
            fin = [sb(f"fin{i}", [P, H]) for i in range(2)]

        consts_loaded, zeroed, prepared = map(sem, ("consts_loaded", "zeroed", "prepared"))
        rows_loaded = [sem(f"rows_loaded{i}") for i in range(2)]
        mask_loaded = [sem(f"mask_loaded{i}") for i in range(2)]
        stored = [sem(f"stored{i}") for i in range(2)]
        J_full = [sem(f"J_full{i}") for i in range(2)]
        J_taken = [sem(f"J_taken{i}") for i in range(2)]
        S_full = [sem(f"S_full{i}") for i in range(SB)]
        S_taken = [sem(f"S_taken{i}") for i in range(SB)]
        O_full, O_taken, T_full, T_taken = map(sem, ("O_full", "O_taken", "T_full", "T_taken"))
        (resid_ready, madd_ready, hT_hi, bank_seen, p_ready, rec_ready, normed,
         aT_hi, q_hi, k_hi, summed, squared, small, guess_ready, newton, root_ready, nrm_ready, scaled, fin_ready) = map(
            sem, ("resid_ready", "madd_ready", "hT_hi", "bank_seen", "p_ready", "rec_ready", "normed",
                  "aT_hi", "q_hi", "k_hi", "summed", "squared", "small", "guess_ready", "newton",
                  "root_ready", "nrm_ready", "scaled", "fin_ready"))

        PER_STEP = dict(J=10 if L == 0 else 6, S=2 * ROUNDS, O=ROUNDS, T=2 - L, entry=1, hT=2,
                        pair=2 * ROUNDS, bank=SB * ROUNDS, q=1, k=1 if L else KC, aT=ROUNDS, done=1, normed=1,
                        newton=4 * NEWTON,
                        small=1 + 1 + 2 * NEWTON if L == 0 else 3 + 1)
        ROW_LOADS = 2 if L == 0 else 3
        CONSTS = 16 * (5 if L == 0 else 6)
        PREPARED = 1 if L == 0 else 3

        u0 = staging.first[2 * L]
        targets = {}
        for u in range(2):
            ks = slice(2 * u, 2 * u + 2)
            targets[u0 + u] = [(whole, [w_[:, ks, :] for w_ in wq])]
            targets[staging.first[2 * L + 1] - 2 + u] = [(whole, [w_[:, ks, :] for w_ in wo])]
        if L == 0:
            def take(n):
                return lambda staged: staged.rearrange("p k (f two) -> p k f two", two=2)[:, :, :, n]
            for k in range(KC):
                targets[u0 + 2 + k] = [(take(n), [w_[:, k:k + 1, :] for w_ in ww]) for n, ww in enumerate((wk, wv))]
        else:
            targets[u0 + 2] = [(whole, [w_[:, :, :] for w_ in wkv])]
        end = staging.first[2 * L + 1]
        WEIGHTS = dict(query=range(u0, u0 + 2), key=range(u0 + 2, end - 2), out=range(end - 2, end))

        def prologue(do):
            do["residual"](0, 0)
            for kind in range(2):
                do["turn"](0, 0, kind)
                do["turn_low"](0, 0, kind)
            do["weights"](WEIGHTS["query"])
            do["weights"](WEIGHTS["key"])
            do["weights_ready"](WEIGHTS["query"])
            do["query"](0, 0)
            do["weights_ready"](WEIGHTS["key"])
            do["key"](0, 0, 0)
            do["turn_query"](0, 0)
            if L == 0:
                do["key"](0, 0, 1)
                do["weights"](WEIGHTS["out"])
                for c in range(2, KC):
                    do["key"](0, 0, c)
            else:
                do["turn_key"](0, 0)
                do["weights"](WEIGHTS["out"])
            do["projected"](0, 0)
            for pair in range(2):
                do["scores"](0, 0, 0, pair)
                do["mask"](0, 0, 0, pair)
            if L == 0:
                for kind in range(2):
                    do["value"](0, 0, kind)
                for j in range(SB):
                    do["exp"](0, 0, 0, j)
            for kind in range(2):
                do["turn"](1, 1, kind)
                do["turn_low"](1, 1, kind)
            if L == 1:
                for j in range(SB):
                    do["exp"](0, 0, 0, j)
            do["residual"](1, 1)

        def first_round(do, b, s, ahead, behind, unfinished):
            o = 1 - s
            def exp(j):
                if behind:
                    do["exp"](b, s, 0, j)

            exp(0)
            exp(1)
            if L == 0 and behind:
                do["probs"](b - 1, o, 1)
            if ahead:
                do["query"](b + 1, o)
            if L == 1 and behind:
                do["probs"](b - 1, o, 1)
            if L == 0:
                exp(2)
            do["normalise"](b, s, 0, 0)
            if L == 1 and ahead:
                do["turn_query"](b + 1, o)
            if L == 1 and unfinished:
                do["norm"](b - 2, s)
                do["affine"](b - 2, s)
            if L == 1:
                exp(2)
            exp(3)
            do["scores"](b, s, 1, 0)
            do["mask"](b, s, 1, 0)
            if L == 0 and ahead:
                do["turn_query"](b + 1, o)
                do["key"](b + 1, o, 0)
            if behind:
                do["values"](b - 1, o, 1)
            do["normalise"](b, s, 0, 1)
            if ahead:
                do["key"](b + 1, o, 1 - L)
            do["scores"](b, s, 1, 1)
            do["mask"](b, s, 1, 1)
            if L == 0 and ahead:
                do["key"](b + 1, o, 2)
                do["key"](b + 1, o, 3)

        def second_round(do, b, s, ahead, turned, behind):
            o = 1 - s
            do["exp"](b, s, 1, 0)
            if L == 0:
                if behind:
                    do["output"](b - 1, o)
                do["exp"](b, s, 1, 1)
                do["probs"](b, s, 0)
                do["exp"](b, s, 1, 2)
                do["normalise"](b, s, 1, 0)
                do["exp"](b, s, 1, 3)
                if behind:
                    do["norm"](b - 1, o)
                if ahead:
                    do["value"](b + 1, o, 0)
                do["normalise"](b, s, 1, 1)
                if behind and ahead:
                    do["residual"](b + 1, o)
                if ahead:
                    do["projected"](b + 1, o)
                    do["scores"](b + 1, o, 0, 0)
                    do["mask"](b + 1, o, 0, 0)
                    do["value"](b + 1, o, 1)
                if turned:
                    do["turn"](b + 2, s, 0)
                if ahead:
                    do["scores"](b + 1, o, 0, 1)
                if turned:
                    do["turn_low"](b + 2, s, 0)
                    do["turn"](b + 2, s, 1)
                if ahead:
                    do["mask"](b + 1, o, 0, 1)
                if turned:
                    do["turn_low"](b + 2, s, 1)
                do["values"](b, s, 0)
                if behind:
                    do["finish"](b - 1, o)
            else:
                if ahead:
                    do["turn_key"](b + 1, o)
                if behind:
                    do["output"](b - 1, o)
                do["exp"](b, s, 1, 1)
                if turned:
                    do["turn"](b + 2, s, 0)
                do["probs"](b, s, 0)
                if turned:
                    do["turn"](b + 2, s, 1)
                do["exp"](b, s, 1, 2)
                do["normalise"](b, s, 1, 0)
                if turned:
                    do["turn_low"](b + 2, s, 0)
                    do["turn_low"](b + 2, s, 1)
                do["exp"](b, s, 1, 3)
                if behind:
                    do["moments"](b - 1, o)
                if ahead:
                    do["projected"](b + 1, o)
                    do["scores"](b + 1, o, 0, 0)
                    do["mask"](b + 1, o, 0, 0)
                do["normalise"](b, s, 1, 1)
                if behind:
                    do["root"](b - 1, o)
                    if ahead:
                        do["residual"](b + 1, o)
                do["values"](b, s, 0)
                if ahead:
                    do["scores"](b + 1, o, 0, 1)
                    do["mask"](b + 1, o, 0, 1)

        def entry(do, b, s, ahead=True, turned=True, unfinished=True):
            first_round(do, b, s, ahead, True, unfinished)
            second_round(do, b, s, ahead, turned, True)

        def all_entries(eng, w, do):
            prologue(do)
            first_round(do, 0, 0, ahead=True, behind=False, unfinished=False)
            do["weights_ready"](WEIGHTS["out"])
            second_round(do, 0, 0, ahead=True, turned=True, behind=False)
            entry(do, 1, 1, unfinished=False)
            with eng.Fori(0, (B - 4) // 2) as it:
                w.enter(it, 2)
                entry(do, it * 2 + 2, 0)
                entry(do, it * 2 + 3, 1)
                w.leave((B - 4) // 2)
            entry(do, B - 2, 0, turned=False)
            entry(do, B - 1, 1, ahead=False, turned=False)
            if L == 1:
                do["norm"](B - 2, 0)
                do["affine"](B - 2, 0)
            do["probs"](B - 1, 1, 1)
            do["values"](B - 1, 1, 1)
            do["output"](B - 1, 1)
            if L == 1:
                do["moments"](B - 1, 1)
                do["root"](B - 1, 1)
            do["norm"](B - 1, 1)
            do["affine"](B - 1, 1)
            do["finish"](B - 1, 1)

        with nc.Block() as block:

            @block.sync
            def _(sp):
                def load_rows(b, s):
                    sp.dma_start(rows[s][:, 0, :], ctx_rows[b]).then_inc(rows_loaded[s], 16)
                    if L == 0:
                        sp.dma_start(rows[s][:, 1, :], x[b]).then_inc(rows_loaded[s], 16)
                    else:
                        for a in range(2):
                            sp.dma_start(rows[s][:, 1, a * 256:(a + 1) * 256],
                                         between[:, 2 * s + a, bass.ds((b - s) * R, 256)])\
                                .then_inc(rows_loaded[s], 16)

                def load_mask(b, s):
                    if L == 0:
                        sp.dma_start(mrow[s][:, :], mask[b].partition_broadcast(P)).then_inc(mask_loaded[s], 16)
                    else:
                        sp.dma_start(madd[s][:, :], mask[b, 0]).then_inc(mask_loaded[s], 16)

                def load_next(b, s):
                    entries, halves, used = b + 1, b * 2 + 2, b * (2 * ROUNDS) + 2
                    if not isinstance(b, int):
                        entries, halves, used = sp.snap(entries), sp.snap(halves), sp.snap(used)
                    sp.wait_ge(resid_ready, entries)
                    sp.wait_ge(hT_hi, halves)
                    load_rows(b + 2, s)
                    if L == 0:
                        sp.wait_ge(madd_ready, b + 1)
                    else:
                        sp.wait_ge(S_taken[SB - 1], used)
                    load_mask(b + 2, s)

                def store(b, s):
                    if L == 1:
                        sp.wait_ge(fin_ready, b + 1)
                        sp.dma_start(out[b], fin[s][:, :]).then_inc(stored[s], 16)

                if L == 1:
                    for s in range(2):
                        sp.nop().then_inc(stored[s], 16)
                def load_weights(us):
                    for u in us:
                        if L == 0 or u not in staging.prefetched(2):
                            staging.load(sp, u)

                load_rows(0, 0)
                load_mask(0, 0)
                load_weights(WEIGHTS["query"])
                vectors = [(bq_all[:, :], q_b), (bo_all[:, :], o_b), (nw_all[:, :], norm_w)]
                if L == 0:
                    vectors += [(bkv_all[:, :], kv_b[0])]
                    sp.dma_start(bk_part[:, :, :], kv_b[0].rearrange("(c p two) -> p c two", p=P, two=2))\
                        .then_inc(consts_loaded, 16)
                else:
                    vectors += [(bkv_all[:, 0:KW], kv_b[0]), (bkv_all[:, KW:2 * KW], kv_b[1]),
                                (nb_all[:, :], norm_b)]
                for to, frm in vectors:
                    sp.dma_start(to, frm.partition_broadcast(P)).then_inc(consts_loaded, 16)
                load_weights(WEIGHTS["key"])
                load_rows(1, 1)
                load_mask(1, 1)
                load_weights(WEIGHTS["out"])
                if L == 0:
                    for u in staging.prefetched(1):
                        staging.load(sp, u)
                load_next(0, 0)
                load_next(1, 1)
                with sp.Fori(0, (B - 4) // 2) as it:
                    for s in range(2):
                        load_next(it * 2 + s + 2, s)
                        store(it * 2 + s, s)
                for b in range(B - 4, B):
                    store(b, b % 2)
                if L == 1:
                    for s in range(2):
                        sp.wait_ge(stored[s], 16 * (B // 2 + 1))

            @block.gpsimd
            def _(pool):
                if L == 0:
                    pool.memset(ident[:, :], 0.0).then_inc(zeroed, 1)
                    for s in range(2):
                        pool.memset(madd[s][:, R:2 * R], 0.0).then_inc(zeroed, 1)
                    pool.wait_ge(zeroed, 3)
                    pool.affine_select(out=ident[:, :], in_=ident[:, :], compare_op=ALU.not_equal,
                                       fill=1.0, base=0, pattern=[[-1, P]], channel_multiplier=1)\
                        .then_inc(prepared, 1)
                else:
                    for s in range(2):
                        pool.memset(V[s][:, :, :, :], 0.0).then_inc(prepared, 1)
                    pool.memset(three_halves[:, :], 1.5).then_inc(prepared, 1)
                    pool.wait_ge(prepared, PREPARED)
                pool.wait_ge(consts_loaded, CONSTS)

                w = Walk(PER_STEP)
                if L == 1:
                    pool.nop().then_inc(scaled, 1)

                def normalise(b, s, r, pair):
                    slot = r % 2
                    pool.wait_ge(rec_ready, w.event("pair"))
                    for j in (2 * pair, 2 * pair + 1):
                        part = pr[slot][:, j, :].rearrange("p (h k) -> p h k", k=keys)
                        by = rec[slot][:, j * per_bank:(j + 1) * per_bank]
                        pool.tensor_tensor(part, part, by.unsqueeze(2).broadcast_to([P, per_bank, keys]),
                                           ALU.mult).then_inc(normed, 1)

                def residual(b, s):
                    _, n = w.use("entry", 2)
                    if not isinstance(b, int) or b >= 2:
                        pool.wait_ge(summed if L else nrm_ready, b - 1)
                    pool.wait_ge(rows_loaded[s], (n + 1) * (16 * ROW_LOADS))
                    pool.tensor_tensor(resid[s][:, :], rows[s][:, 1, :], bo_all[:, :], ALU.add)\
                        .then_inc(resid_ready, 1)

                def root(b, s):
                    y, t, h = (stat[:, c:c + 1] for c in (2, 3, 10))
                    pool.wait_ge(guess_ready, b + 1)
                    for _ in range(NEWTON):
                        for to, in0, in1, op in ((t, y, y, ALU.mult), (t, t, h, ALU.mult),
                                                 (t, t, three_halves[:, :], ALU.add), (y, y, t, ALU.mult)):
                            pool.tensor_tensor(to, in0, in1, op).then_inc(newton, 1)
                            pool.wait_ge(newton, w.event("newton"))
                    pool.nop().then_inc(root_ready, 1)

                def affine(b, s):
                    if L == 1:
                        _, n = w.use("done", 2)
                        pool.wait_ge(nrm_ready, b + 1)
                        pool.wait_ge(stored[s], (n + 1) * 16)
                        pool.tensor_tensor(fin[s][:, :], nrm[:, :], nw_all[:, :], ALU.mult).then_inc(scaled, 1)
                        pool.wait_ge(scaled, b + 2)
                        pool.tensor_tensor(fin[s][:, :], fin[s][:, :], nb_all[:, :], ALU.add)\
                            .then_inc(fin_ready, 1)

                def other(*_):
                    pass

                all_entries(pool, w, dict(normalise=normalise, residual=residual, norm=other, root=root, affine=affine, turn=other,
                                          weights=other, weights_ready=other, query=other, key=other, turn_query=other,
                                          turn_key=other, value=other, scores=other, exp=other, probs=other,
                                          values=other, output=other, finish=other, mask=other,
                                          projected=other, turn_low=other, moments=other))

            @block.scalar
            def _(act):
                w = Walk(PER_STEP)

                def weights(us):
                    for u in us:
                        staging.take_hi(nc, act, u, targets[u])

                def turn(b, s, kind):
                    j, n = w.use("J", 2)
                    act.wait_ge(J_full[j], n + 1)
                    nc.scalar.activation(hT[0][:, :, kind, :], J[j][:, :].rearrange("p (k r) -> p k r", k=KC),
                                         ACT.Copy).then_inc(hT_hi, 1)

                def query(b, s):
                    w.use("J")

                def key(b, s, c):
                    j, n = w.use("J", 2)
                    if L == 0:
                        if isinstance(b, int) and b == 0 and c == 0:
                            act.wait_ge(consts_loaded, CONSTS)
                        act.wait_ge(J_full[j], n + 1)
                        nc.scalar.activation(KT[s][0][:, c, :], J[j][:, 0:keys], ACT.Identity,
                                             bias=bk_part[:, c, 0:1]).then_inc(k_hi, 1)

                def value(b, s, kind):
                    w.use("J")

                def turn_query(b, s):
                    _, n = w.use("T")
                    act.wait_ge(T_full, n + 1)
                    nc.scalar.activation(QT[s][0][:, :, :], T[:, :].rearrange("p (k r) -> p k r", k=KC),
                                         ACT.Copy, scale=scale).then_inc(q_hi, 1)

                def turn_key(b, s):
                    j, n = w.use("J", 2)
                    act.wait_ge(zeroed, 2)
                    act.wait_ge(J_full[j], n + 1)
                    for a in range(2):
                        last = nc.scalar.activation(KT[s][0][:, a, :], J[j][:, 0:R], ACT.Copy,
                                                    scale=parity[:, a:a + 1])
                    last.then_inc(k_hi, 1)

                def scores(b, s, r, pair):
                    if pair == 0:
                        w.use("S")

                scored = {}

                def exp(b, s, r, j):
                    slot = r % 2
                    if j == 0:
                        scored[r] = w.so_far("S")
                    act.wait_ge(S_taken[j], scored[r])
                    for h in range(per_bank):
                        part = pr[slot][:, j, h * keys:(h + 1) * keys]
                        at = slice(j * per_bank + h, j * per_bank + h + 1)
                        last = nc.scalar.activation(part, part, ACT.Exp, bias=nmax[slot][:, at], scale=-1.0,
                                                    accum_out=den[slot][:, at])
                    last.then_inc(p_ready, 1)

                def probs(b, s, r):
                    _, n = w.use("S")
                    for j in range(1, SB, 2):
                        act.wait_ge(S_full[j], n + 1)
                        nc.scalar.activation(pT[:, j, :], S[j][:, :], ACT.Copy).then_inc(S_taken[j], 1)

                def output(b, s):
                    j, n = w.use("J", 2)
                    if L == 0:
                        act.wait_ge(J_taken[j], n + 1)
                        nc.scalar.activation(nrm[:, :], res[:, :], ACT.Square, accum_out=stat[:, 0:1])\
                            .then_inc(squared, 1)

                def finish(b, s):
                    if L == 0:
                        _, n = w.use("T")
                        act.wait_ge(T_full, n + 1)
                        nc.scalar.activation(between[:, :, bass.ds(b * R, R)],
                                             T[:, :].rearrange("p (k r) -> p k r", k=KC),
                                             ACT.Copy).then_inc(T_taken, 1)

                def other(*_):
                    pass

                all_entries(act, w, dict(weights=weights, weights_ready=other, turn=turn, query=query, key=key, value=value,
                                         turn_query=turn_query, turn_key=turn_key, scores=scores, exp=exp,
                                         probs=probs, output=output, finish=finish, normalise=other,
                                         values=other, norm=other, residual=other, mask=other, projected=other,
                                         turn_low=other, affine=other, root=other, moments=other))

            @block.vector
            def _(dve):
                w = Walk(PER_STEP)
                if L == 1:
                    halves = ident[:, :].rearrange("p (m a d) -> p a m d", a=2, d=DH1)
                    for a in range(2):
                        last = nc.vector.tensor_reduce(parity[:, a:a + 1], halves[:, a], AX.XY, ALU.add)
                        last.then_inc(zeroed, 1)
                def weights(us):
                    for u in us:
                        staging.take_lo(nc, dve, u, targets[u])

                low = {}

                def turn(b, s, kind):
                    low[kind] = w.use("J", 2)

                def turn_low(b, s, kind):
                    if L == 0 and kind == 0:
                        _, n = w.use("entry", 2)
                        dve.wait_ge(mask_loaded[s], (n + 1) * 16)
                        nc.vector.tensor_scalar(madd[s][:, 0:R], mrow[s][:, :], 0.0, NEG, ALU.is_equal,
                                                ALU.mult).then_inc(madd_ready, 1)
                    j, n = low[kind]
                    dve.wait_ge(J_full[j], n + 1)
                    dve.wait_ge(hT_hi, w.event("hT"))
                    nc.vector.tensor_tensor(hT[1][:, :, kind, :], J[j][:, :].rearrange("p (k r) -> p k r", k=KC),
                                            hT[0][:, :, kind, :].bitcast(F32), ALU.subtract)\
                        .then_inc(J_taken[j], 1)

                def query(b, s):
                    j, n = w.use("J", 2)
                    if isinstance(b, int) and b == 0:
                        dve.wait_ge(consts_loaded, CONSTS)
                        dve.wait_ge(prepared, PREPARED)
                    dve.wait_ge(J_full[j], n + 1)
                    if L == 0:
                        nc.vector.tensor_tensor(Qn[:, :], J[j][:, :], bq_all[:, :], ALU.add)\
                            .then_inc(J_taken[j], 1)
                    else:
                        def by_group(t):
                            return t[:, :].rearrange("p (g c d) -> p g c d", c=GROUPS1, d=DH1)
                        nc.vector.tensor_tensor(Qn[:, :].rearrange("p (c g d) -> p g c d", c=GROUPS1, d=DH1),
                                                by_group(J[j]), by_group(bq_all), ALU.add)\
                            .then_inc(J_taken[j], 1)

                def key(b, s, c):
                    j, n = w.use("J", 2)
                    if L == 1:
                        dve.wait_ge(J_full[j], n + 1)
                        nc.vector.tensor_tensor(Kn[:, :], J[j][:, 0:KW], bkv_all[:, 0:KW], ALU.add)
                        for a in range(2):
                            def heads(t):
                                return t[:, KW:2 * KW].rearrange("p (m a d) -> p a m d", a=2, d=DH1)[:, a]
                            last = nc.vector.tensor_tensor(V[s][:, :, a, a * DH1:(a + 1) * DH1],
                                                           heads(J[j]), heads(bkv_all), ALU.add)
                        last.then_inc(J_taken[j], 1)
                    else:
                        dve.wait_ge(J_full[j], n + 1)
                        dve.wait_ge(k_hi, w.event("k"))
                        nc.vector.scalar_tensor_tensor(KT[s][1][:, c, :], J[j][:, 0:keys], bk_part[:, c, 0:1],
                                                       KT[s][0][:, c, :].bitcast(F32), ALU.add, ALU.subtract)\
                            .then_inc(J_taken[j], 1)

                def value(b, s, kind):
                    j, n = w.use("J", 2)
                    dve.wait_ge(J_full[j], n + 1)
                    nc.vector.tensor_tensor(V[s][:, kind, :], J[j][:, :],
                                            bkv_all[:, :].rearrange("p (f two) -> p f two", two=2)[:, :, 1],
                                            ALU.add).then_inc(J_taken[j], 1)

                def turn_query(b, s):
                    _, n = w.use("T")
                    dve.wait_ge(T_full, n + 1)
                    dve.wait_ge(q_hi, w.event("q"))
                    nc.vector.scalar_tensor_tensor(QT[s][1][:, :, :], T[:, :].rearrange("p (k r) -> p k r", k=KC),
                                                   scale, QT[s][0][:, :, :].bitcast(F32), ALU.mult, ALU.subtract)\
                        .then_inc(T_taken, 1)

                def turn_key(b, s):
                    j, n = w.use("J", 2)
                    dve.wait_ge(J_full[j], n + 1)
                    dve.wait_ge(k_hi, w.event("k"))
                    for a in range(2):
                        last = nc.vector.scalar_tensor_tensor(
                            KT[s][1][:, a, :], J[j][:, 0:R], parity[:, a:a + 1],
                            KT[s][0][:, a, :].bitcast(F32), ALU.mult, ALU.subtract)
                    last.then_inc(J_taken[j], 1)

                scored = {}

                def scores(b, s, r, pair):
                    if pair == 0:
                        _, scored[r] = w.use("S")

                def mask(b, s, r, pair):
                    slot, n = r % 2, scored[r]
                    if r == 0 and pair == 0:
                        if L == 0:
                            dve.wait_ge(madd_ready, b + 1)
                        else:
                            _, m = w.use("entry", 2)
                            dve.wait_ge(mask_loaded[s], (m + 1) * 16)
                        dve.nop().then_inc(bank_seen, 1)
                    for j in (2 * pair, 2 * pair + 1):
                        dve.wait_ge(S_full[j], n + 1)
                        dve.nop().then_inc(bank_seen, 1)
                        for h in range(per_bank):
                            cols = slice(h * keys, (h + 1) * keys)
                            last = nc.vector.tensor_tensor_reduce(
                                pr[slot][:, j, cols], S[j][:, cols], madd[s][:, :], -1.0, FAR, ALU.add,
                                ALU.min, nmax[slot][:, j * per_bank + h:j * per_bank + h + 1])
                        last.then_inc(S_taken[j], 1)

                def normalise(b, s, r, pair):
                    slot = r % 2
                    sums = slice(pair * 2 * per_bank, (pair + 1) * 2 * per_bank)
                    for j in range(2):
                        last = w.event("bank")
                    dve.wait_ge(p_ready, last)
                    nc.vector.reciprocal(rec[slot][:, sums], den[slot][:, sums]).then_inc(rec_ready, 1)

                def probs(b, s, r):
                    _, n = w.use("S")
                    for j in range(0, SB, 2):
                        dve.wait_ge(S_full[j], n + 1)
                        nc.vector.tensor_copy(pT[:, j, :], S[j][:, :]).then_inc(S_taken[j], 1)

                def values(b, s, r):
                    hi, lo = (t[:, RC * r:RC * (r + 1), :] for t in aT[s if L else 0])
                    result = O[:, 0:RC * R].rearrange("p (c r) -> p c r", c=RC)
                    _, n = w.use("O")
                    dve.wait_ge(O_full, n + 1)
                    nc.vector.tensor_copy(hi, result).then_inc(aT_hi, 1)
                    dve.wait_ge(aT_hi, w.event("aT"))
                    nc.vector.tensor_tensor(lo, result, hi.bitcast(F32), ALU.subtract).then_inc(O_taken, 1)

                added = []

                def output(b, s):
                    j, n = w.use("J", 2)
                    added[:] = [(J_taken[j], n + 1)]
                    dve.wait_ge(resid_ready, b + 1)
                    dve.wait_ge(J_full[j], n + 1)
                    nc.vector.tensor_tensor(res[:, :], J[j][:, :], resid[s][:, :], ALU.add)\
                        .then_inc(J_taken[j], 1)

                def guess():
                    m, y, t, h = (stat[:, c:c + 1] for c in (1, 2, 3, 10))
                    nc.vector.tensor_scalar(h, m, -0.5, None, ALU.mult)
                    nc.vector.tensor_scalar(t.bitcast(I32), m.bitcast(I32), 1, None, ALU.logical_shift_right)\
                        .then_inc(small, 1)
                    dve.wait_ge(small, w.event("small"))
                    nc.vector.tensor_scalar(y.bitcast(I32), t.bitcast(I32), -1.0, float(0x5F3759DF), ALU.mult,
                                            ALU.add).then_inc(guess_ready, 1)

                def newton_steps():
                    y, t, h = (stat[:, c:c + 1] for c in (2, 3, 10))
                    for _ in range(NEWTON):
                        nc.vector.scalar_tensor_tensor(t, y, h, y, ALU.mult, ALU.mult).then_inc(small, 1)
                        dve.wait_ge(small, w.event("small"))
                        nc.vector.scalar_tensor_tensor(y, t, 1.5, y, ALU.add, ALU.mult).then_inc(small, 1)
                        dve.wait_ge(small, w.event("small"))

                def moments(b, s):
                    if L == 1:
                        dve.wait_ge(*added[0])
                        nc.vector.bn_stats(stat[:, 4:10], res[:, :]).then_inc(summed, 1)
                        dve.wait_ge(summed, b + 1)
                        mean_e, var_e, mean_o, var_o, gap, var = (
                            stat[:, c:c + 1] for c in (5, 6, 8, 9, 11, 12))
                        nc.vector.tensor_tensor(stat[:, 0:1], mean_e, mean_o, ALU.add)
                        nc.vector.scalar_tensor_tensor(var, var_e, H * EPS, var_o, ALU.add, ALU.add)
                        nc.vector.tensor_tensor(gap, mean_e, mean_o, ALU.subtract).then_inc(small, 1)
                        dve.wait_ge(small, w.event("small"))
                        nc.vector.tensor_scalar(stat[:, 0:1], stat[:, 0:1], 0.5, None, ALU.mult)
                        nc.vector.scalar_tensor_tensor(stat[:, 13:14], gap, 0.25, gap, ALU.mult, ALU.mult)\
                            .then_inc(small, 1)
                        dve.wait_ge(small, w.event("small"))
                        nc.vector.scalar_tensor_tensor(stat[:, 1:2], var, 1.0 / H, stat[:, 13:14], ALU.mult,
                                                       ALU.add).then_inc(small, 1)
                        dve.wait_ge(small, w.event("small"))
                        guess()

                def norm(b, s):
                    done = w.event("normed")
                    if L == 0:
                        dve.wait_ge(squared, done)
                        nc.vector.tensor_scalar(stat[:, 1:2], stat[:, 0:1], 1.0 / H, EPS, ALU.mult, ALU.add)\
                            .then_inc(small, 1)
                        dve.wait_ge(small, w.event("small"))
                        guess()
                        dve.wait_ge(guess_ready, done)
                        newton_steps()
                        nc.vector.scalar_tensor_tensor(nrm[:, :], res[:, :], stat[:, 2:3], nw_all[:, :],
                                                       ALU.mult, ALU.mult).then_inc(nrm_ready, 1)
                    else:
                        dve.wait_ge(root_ready, done)
                        dve.wait_ge(scaled, done)
                        nc.vector.tensor_scalar(nrm[:, :], res[:, :], stat[:, 0:1], stat[:, 2:3],
                                                ALU.subtract, ALU.mult).then_inc(nrm_ready, 1)

                def finish(b, s):
                    if L == 0:
                        w.use("T")

                def other(*_):
                    pass

                all_entries(dve, w, dict(weights=weights, weights_ready=other, turn=turn, query=query, key=key, value=value,
                                         turn_query=turn_query, turn_key=turn_key, scores=scores,
                                         normalise=normalise, probs=probs, values=values, output=output,
                                         norm=norm, finish=finish, exp=other, residual=other, mask=mask,
                                         projected=other, turn_low=turn_low, affine=other, root=other, moments=moments))

            @block.tensor
            def _(pe):
                w = Walk(PER_STEP)
                if L == 0:
                    pe.wait_ge(prepared, PREPARED)

                def weights_ready(us):
                    pe.wait_ge(staging.split, staging.splits(us[-1] + 1))

                def turn(b, s, kind):
                    if kind == 0:
                        _, e = w.use("entry", 2)
                        pe.wait_ge(rows_loaded[s], (e + 1) * (16 * ROW_LOADS))
                    j, n = w.use("J", 2)
                    pe.wait_ge(J_taken[j], n)
                    for k in range(KC):
                        mm = nc.tensor.transpose(J[j][:, k * R:(k + 1) * R], rows[s][:, kind, k * P:(k + 1) * P],
                                                 ident[:, :])
                    mm.then_inc(J_full[j], 1)

                natural = {}

                def query(b, s):
                    for i in range(2):
                        pe.wait_ge(J_taken[i], w.so_far("J", 2, i))
                    j, n = w.use("J", 2)
                    natural["query"] = (J_taken[j], n + 1)
                    pe.wait_ge(J_taken[j], n)
                    split_product(nc, J[j][:, :], lambda h, k: hT[h][:, k, 1, :], lambda h, k: wq[h][:, k, :], KC)\
                        .then_inc(J_full[j], 1)

                def key(b, s, c):
                    j, n = w.use("J", 2)
                    natural["key"] = natural[c % 2] = (J_taken[j], n + 1)
                    pe.wait_ge(J_taken[j], n)
                    if L == 0:
                        mm = split_product(nc, J[j][:, 0:keys], lambda h, k: wk[h][:, k, c * P:(c + 1) * P],
                                           lambda h, k: hT[h][:, k, :, :], KC)
                    else:
                        mm = split_product(nc, J[j][:, 0:2 * KW], lambda h, k: hT[h][:, k, 0, :],
                                           lambda h, k: wkv[h][:, k, :], KC)
                    mm.then_inc(J_full[j], 1)

                def value(b, s, kind):
                    j, n = w.use("J", 2)
                    pe.wait_ge(J_taken[j], n)
                    split_product(nc, J[j][:, :], lambda h, k: hT[h][:, k, kind, :],
                                  lambda h, k: wv[h][:, k, :], KC).then_inc(J_full[j], 1)

                def turn_query(b, s):
                    pe.wait_ge(*natural["query"])
                    _, n = w.use("T")
                    natural["turned"] = (T_taken, n + 1)
                    pe.wait_ge(T_taken, n)
                    for c in range(KC):
                        mm = nc.tensor.transpose(T[:, c * R:(c + 1) * R], Qn[:, c * P:(c + 1) * P], ident[:, :])
                    mm.then_inc(T_full, 1)

                def turn_key(b, s):
                    pe.wait_ge(*natural["key"])
                    j, n = w.use("J", 2)
                    natural[0] = natural[1] = (J_taken[j], n + 1)
                    pe.wait_ge(J_taken[j], n)
                    nc.tensor.transpose(J[j][:, 0:R], Kn[:, :], ident[:, :]).then_inc(J_full[j], 1)

                def projected(b, s):
                    for name in ("turned", 0, 1):
                        pe.wait_ge(*natural[name])

                scored = {}

                def scores(b, s, r, pair):
                    if pair == 0:
                        _, scored[r] = w.use("S")
                    n = scored[r]
                    banks = (2 * pair, 2 * pair + 1)
                    for j in banks:
                        pe.wait_ge(S_taken[j], n)
                    for c in range(RC):
                        for qh, kh in PASSES:
                            for j in banks:
                                strip = slice(32 * j, 32 * (j + 1))
                                k_ap = KT[s][kh][strip, RC * r + c, :] if L == 0 else KT[s][kh][strip, :, :]
                                mm = nc.tensor.matmul(S[j][:, c * 256:(c + 1) * 256],
                                                      QT[s][qh][strip, RC * r + c, :], k_ap,
                                                      start=(qh, kh) == PASSES[0], stop=(qh, kh) == PASSES[-1])
                                if c == RC - 1 and (qh, kh) == PASSES[-1]:
                                    mm.then_inc(S_full[j], 1)

                turned = {}

                def probs(b, s, r):
                    slot = r % 2
                    _, n = w.use("S")
                    turned[r] = n
                    for j in range(SB):
                        pe.wait_ge(normed, w.event("bank"))
                        pe.wait_ge(S_taken[j], n)
                        for q in range(4):
                            to = q if L == 0 else (q % 2) * 2 + q // 2
                            mm = nc.tensor.transpose(S[j][:, to * P:(to + 1) * P],
                                                     pr[slot][:, j, q * P:(q + 1) * P], ident[:, :])
                        mm.then_inc(S_full[j], 1)

                def values(b, s, r):
                    _, n = w.use("O")
                    pe.wait_ge(O_taken, n)
                    for j in range(SB):
                        pe.wait_ge(S_taken[j], turned[r] + 1)
                    if L == 0:
                        for c in range(RC):
                            for kind in range(2):
                                for j in range(SB):
                                    head = 4 * (RC * r + c) + j
                                    at = (c * 2 + kind) * R
                                    mm = nc.tensor.matmul(O[32 * j:32 * (j + 1), c * R:(c + 1) * R],
                                                          V[s][:, kind, head * DH0:(head + 1) * DH0],
                                                          pT[:, j, at:at + R], start=kind == 0, stop=kind == 1)
                    else:
                        for a in range(2):
                            for j in range(SB):
                                mm = nc.tensor.matmul(O[32 * j:32 * (j + 1), 0:RC * R], V[s][:, j, a, :],
                                                      pT[:, j, a * RC * R:(a + 1) * RC * R],
                                                      start=a == 0, stop=a == 1)
                    mm.then_inc(O_full, 1)

                def output(b, s):
                    pe.wait_ge(O_taken, w.event("done") * ROUNDS)
                    j, n = w.use("J", 2)
                    pe.wait_ge(J_taken[j], n)
                    split_product(nc, J[j][:, :], lambda h, k: aT[s if L else 0][h][:, k, :], lambda h, k: wo[h][:, k, :], KC)\
                        .then_inc(J_full[j], 1)

                def finish(b, s):
                    if L == 0:
                        _, n = w.use("T")
                        pe.wait_ge(T_taken, n)
                        pe.wait_ge(nrm_ready, w.so_far("done"))
                        for k in range(KC):
                            mm = nc.tensor.transpose(T[:, k * R:(k + 1) * R], nrm[:, k * P:(k + 1) * P], ident[:, :])
                        mm.then_inc(T_full, 1)

                def other(*_):
                    pass

                all_entries(pe, w, dict(weights=other, weights_ready=weights_ready, turn=turn, query=query, key=key, value=value,
                                        turn_query=turn_query, turn_key=turn_key, scores=scores,
                                        probs=probs, values=values, output=output, finish=finish,
                                        normalise=other, exp=other, norm=other, residual=other,
                                        mask=other, projected=projected, turn_low=other, affine=other, root=other, moments=other))


def mlp(nc, top, staging, between, S, J, x, b1, b2):
    PAIRS, PR = B // 2, 2 * R
    LAG = 2
    RING = 4
    st = ExitStack()

    def sb(name, shape, dt=F32):
        return st.enter_context(nc.sbuf_tensor(f"{name}_m", shape, dt))

    def sem(name):
        return top.enter_context(nc.semaphore(f"{name}_m"))

    with st:
        up = [sb(f"up{h}", [P, KC, FF], F32R) for h in HALVES]
        down = [sb(f"down{h}", [P, FC, H], F32R) for h in HALVES]
        b1_part = sb("b1_part", [P, FC, 1])
        b2_all = sb("b2_all", [P, H])
        nT = [[sb(f"nT{i}{h}", [P, KC, PR], F32R) for h in HALVES] for i in range(2)]
        g = [sb(f"g{i}", [P, PR]) for i in range(RING)]
        gs = [[sb(f"g{i}{h}", [P, PR], F32R) for h in HALVES] for i in range(RING)]
        resid = [sb(f"resid{t}", [P, H]) for t in range(2)]

        consts_loaded = sem("consts_loaded")
        J_full = [sem(f"J_full{i}") for i in range(2)]
        J_taken = [sem(f"J_taken{i}") for i in range(2)]
        A_full = [sem(f"A_full{i}") for i in range(4)]
        A_taken = [sem(f"A_taken{i}") for i in range(4)]
        resid_loaded = [sem(f"resid_loaded{t}") for t in range(2)]
        resid_ready = [sem(f"resid_ready{t}") for t in range(2)]
        n_hi, n_split, g_hi, g_split = map(sem, ("n_hi", "n_split", "g_hi", "g_split"))

        PER_PAIR = dict(J=FC, g=FC, pair=1, n=1)

        u0 = staging.first[1]
        targets = {}
        for v in range(FC // 2):
            targets[u0 + 2 * v] = [(whole, [w_[:, :, v * 2 * P:(v + 1) * 2 * P] for w_ in up])]
            targets[u0 + 2 * v + 1] = [(whole, [w_[:, 2 * v:2 * v + 2, :] for w_ in down])]
        EARLY = 4

        def all_pairs(eng, w, prepare, pair):
            prepare(0, 0)
            pair(0, 0, True, True)
            with eng.Fori(0, (PAIRS - 2) // 2) as it:
                w.enter(it, 2)
                pair(it * 2 + 1, 1, True, False)
                pair(it * 2 + 2, 0, True, False)
                w.leave((PAIRS - 2) // 2)
            pair(PAIRS - 1, 1, False, False)

        with nc.Block() as block:

            @block.sync
            def _(sp):
                with nc.allow_non_contiguous_dma(reason="2048 bias values, one per partition and chunk"):
                    sp.dma_start(b1_part[:, :, :], b1.rearrange("(c p a) -> p c a", p=P, a=1))\
                        .then_inc(consts_loaded, 16)
                sp.dma_start(b2_all[:, :], b2.partition_broadcast(P)).then_inc(consts_loaded, 16)
                for r in range(2):
                    sp.dma_start(resid[r][:, :], x[r]).then_inc(resid_loaded[r], 16)
                for u in range(staging.first[1], staging.first[2]):
                    if u not in staging.prefetched(1):
                        staging.load(sp, u)
                def load_residual(i, t, taken):
                    for r in range(2):
                        sp.wait_ge(A_taken[2 * (1 - t) + r], taken)
                        sp.dma_start(resid[r][:, :], x[i * 2 + r]).then_inc(resid_loaded[r], 16)

                with sp.Fori(0, (PAIRS - 2) // 2) as it:
                    load_residual(it * 2 + 1, 1, it + 2)
                    load_residual(it * 2 + 2, 0, it + 2)
                load_residual(PAIRS - 1, 1, PAIRS // 2 + 1)
                for u in staging.prefetched(2):
                    staging.load(sp, u)

            @block.gpsimd
            def _(pool):
                pool.wait_ge(consts_loaded, 32)
                with pool.Fori(0, PAIRS) as i:
                    for t in range(2):
                        pool.wait_ge(resid_loaded[t], i * 16 + 16)
                        pool.tensor_tensor(resid[t][:, :], resid[t][:, :], b2_all[:, :], ALU.add)\
                            .then_inc(resid_ready[t], 1)

            @block.scalar
            def _(act):
                w = Walk(PER_PAIR)

                def prepare(i, t):
                    nc.scalar.activation(nT[t][0][:, :, :], between[:, :, bass.ds(i * PR, PR)], ACT.Copy)\
                        .then_inc(n_hi, 1)

                def pair(i, t, ahead, first):
                    if first:
                        for u in range(EARLY):
                            staging.take_hi(nc, act, u0 + u, targets[u0 + u])
                        act.wait_ge(consts_loaded, 32)
                    for f in range(FC):
                        if first and f + EARLY < 2 * (FC // 2):
                            staging.take_hi(nc, act, u0 + f + EARLY, targets[u0 + f + EARLY])
                        j, n = w.use("J", 2)
                        slot = f % RING
                        act.wait_ge(J_full[j], n + 1)
                        nc.scalar.activation(g[slot][:, :], J[j][:, 0:PR], ACT.Gelu_apprx_tanh,
                                             bias=b1_part[:, f, :]).then_inc(J_taken[j], 1)
                        act.wait_ge(J_taken[j], n + 1)
                        nc.scalar.activation(gs[slot][0][:, :], g[slot][:, :], ACT.Copy).then_inc(g_hi, 1)
                        if ahead and f == FC // 2:
                            prepare(i + 1, 1 - t)

                all_pairs(act, w, prepare, pair)

            @block.vector
            def _(dve):
                w = Walk(PER_PAIR)
                for bank in range(SB):
                    dve.nop().then_inc(A_taken[bank], 1)

                def prepare(i, t):
                    dve.wait_ge(n_hi, w.event("n"))
                    nc.vector.tensor_tensor(nT[t][1][:, :, :], between[:, :, bass.ds(i * PR, PR)],
                                            nT[t][0][:, :, :].bitcast(F32), ALU.subtract).then_inc(n_split, 1)

                def pair(i, t, ahead, first):
                    if first:
                        for u in range(EARLY):
                            staging.take_lo(nc, dve, u0 + u, targets[u0 + u])
                    for f in range(FC):
                        if first and f + EARLY < 2 * (FC // 2):
                            staging.take_lo(nc, dve, u0 + f + EARLY, targets[u0 + f + EARLY])
                        slot = f % RING
                        dve.wait_ge(g_hi, w.event("g"))
                        nc.vector.tensor_tensor(gs[slot][1][:, :], g[slot][:, :], gs[slot][0][:, :].bitcast(F32),
                                                ALU.subtract).then_inc(g_split, 1)
                        if ahead and f == FC // 2:
                            prepare(i + 1, 1 - t)
                    _, n = w.use("pair", 2)
                    for r in range(2):
                        bank = 2 * t + r
                        dve.wait_ge(resid_ready[r], i + 1)
                        dve.wait_ge(A_full[bank], n + 1)
                        nc.vector.tensor_tensor(between[:, 2 * r:2 * r + 2, bass.ds(i * PR, PR)],
                                                S[bank][:, :].rearrange("p (a c) -> p a c", a=2),
                                                resid[r][:, :].rearrange("p (a c) -> p a c", a=2), ALU.add)\
                            .then_inc(A_taken[bank], 1)

                all_pairs(dve, w, prepare, pair)

            @block.tensor
            def _(pe):
                w = Walk(PER_PAIR)

                def prepare(i, t):
                    pass

                def pair(i, t, ahead, first):
                    _, m = w.use("pair", 2)
                    pe.wait_ge(n_split, i + 1)

                    def up_product(f):
                        j, n = w.use("J", 2)
                        pe.wait_ge(J_taken[j], n)
                        if first:
                            pe.wait_ge(staging.split, staging.splits(u0 + 2 * (f // 2) + 1))
                        split_product(nc, J[j][:, 0:PR], lambda h, k: up[h][:, k, f * P:(f + 1) * P],
                                      lambda h, k: nT[t][h][:, k, :], KC).then_inc(J_full[j], 1)

                    for f in range(LAG):
                        up_product(f)
                    for f in range(FC):
                        if f + LAG < FC:
                            up_product(f + LAG)
                        pe.wait_ge(g_split, w.event("g"))
                        if first:
                            pe.wait_ge(staging.split, staging.splits(u0 + 2 * (f // 2) + 2))
                        for r in range(2):
                            bank = 2 * t + r
                            if f == 0:
                                pe.wait_ge(A_taken[bank], m + 1)
                            mm = split_product(nc, S[bank][:, :],
                                               lambda h, k: gs[f % RING][h][:, r * R:(r + 1) * R],
                                               lambda h, k: down[h][:, f, :], 1, f == 0, f == FC - 1)
                            if f == FC - 1:
                                mm.then_inc(A_full[bank], 1)

                all_pairs(pe, w, prepare, pair)


_INS = ["x", "ctx_2048", "mask_BxS2_ik0", "mask_Bx1xSxS2_ff0", "L0_xattn_q_w", "L0_xattn_q_b",
        "L0_xattn_kv_w", "L0_xattn_kv_b", "L0_xattn_out_w", "L0_xattn_out_b", "L0_xattn_postnorm_w",
        "L0_xattn_mlp_w1", "L0_xattn_mlp_b1", "L0_xattn_mlp_w2", "L0_xattn_mlp_b2",
        "L1_xattn_Wq", "L1_xattn_bq", "L1_xattn_Wk", "L1_xattn_bk", "L1_xattn_Wv", "L1_xattn_bv",
        "L1_xattn_Wo", "L1_xattn_bo", "L1_xattn_gamma", "L1_xattn_beta"]
_OUTS = [((B, R, H), "float32")]


def kernel(**inputs):
    import numpy as _np
    import concourse.bacc as _bacc
    from concourse import mybir as _mybir
    from concourse.bass_utils import run_bass_kernel_spmd as _run

    nc = _bacc.Bacc("TRN2", target_bir_lowering=False, num_devices=1)
    arrays, args = {}, []
    for name in _INS:
        a = _np.ascontiguousarray(inputs[name])
        arrays[f"in_{name}"] = a
        args.append(nc.dram_tensor(f"in_{name}", a.shape, _mybir.dt.from_np(a.dtype), kind="ExternalInput").ap())
    for i, (shape, dtype) in enumerate(_OUTS):
        dt = _mybir.dt.from_np(_np.dtype(dtype))
        args.append(nc.dram_tensor(f"out_{i}", shape, dt, kind="ExternalOutput").ap())
    xattn_kernel(nc, *args)
    r = _run(nc, [arrays], core_ids=[0])
    return r.results[0]["out_0"]
```
